# Optimizing a Trainium2 kernel written in Bass

```python
import numpy as np
import jax
import jax.numpy as jnp

def _softmax(x, axis=-1):
    return jax.nn.softmax(x, axis=axis)

def _gelu(x):
    return jax.nn.gelu(x, approximate=True)

def _silu(x):
    return jax.nn.silu(x)

def _sigmoid(x):
    return jax.nn.sigmoid(x)

def _layernorm(x, axis=-1, eps=1e-05):
    m = jnp.mean(x, axis=axis, keepdims=True)
    v = jnp.var(x, axis=axis, keepdims=True)
    return (x - m) / jnp.sqrt(v + eps)

def _scatter_add(tgt, idx, src, axis=0):
    return tgt.at[idx].add(src)

def _segment_sum(src, seg, n):
    return jax.ops.segment_sum(src, seg, n)
kernel_name = 'mk_seq_preln_d1_jaxref_r8_752ed8'

def setup_inputs(seed: int=0):
    np.random.seed(seed)
    _w = jnp.asarray

    def _L0_attn_setup():
        import jax, jax.numpy as jnp
        import numpy as np
        B, L, D, F = (4, 512, 128, 64)

        def _reference_tuple_inner(x, W_spec, W_decay, b_decay, freqs, W_out):
            Bb, Ll, _ = x.shape
            nf = freqs.shape[0]
            decay = jax.nn.sigmoid(jnp.einsum('bld,df->blf', x, W_decay) + b_decay)
            omega = freqs * 0.1
            rot = jnp.cos(omega) + 1j * jnp.sin(omega)
            spectral = jnp.einsum('bld,df->blf', x, W_spec)
            u = (spectral[..., :nf] + 1j * spectral[..., nf:]).astype(jnp.complex64)
            a = decay.astype(jnp.complex64) * rot

            def step(h, au):
                a_t, u_t = au
                h = a_t * h + u_t
                return (h, h)
            h0 = jnp.zeros((Bb, nf), dtype=jnp.complex64)
            a_t = jnp.transpose(a, (1, 0, 2))
            u_t = jnp.transpose(u, (1, 0, 2))
            h_final, hs = jax.lax.scan(step, h0, (a_t, u_t))
            hs = jnp.transpose(hs, (1, 0, 2))
            y = jnp.concatenate([hs.real, hs.imag], axis=-1)
            out = jnp.einsum('blf,fd->bld', y, W_out)
            return (out, (h_final.real, h_final.imag))
        key = jax.random.key(seed)
        ks = jax.random.split(key, 6)
        scale = 1.0 / np.sqrt(D)
        return {'x': jax.random.normal(ks[0], (B, L, D), dtype=jnp.float32), 'W_spec': jax.random.normal(ks[1], (D, 2 * F), dtype=jnp.float32) * scale, 'W_decay': jax.random.normal(ks[2], (D, F), dtype=jnp.float32) * scale, 'b_decay': jax.random.normal(ks[3], (F,), dtype=jnp.float32) * 0.02, 'freqs': jax.random.normal(ks[4], (F,), dtype=jnp.float32), 'W_out': jax.random.normal(ks[5], (2 * F, D), dtype=jnp.float32) * (1.0 / np.sqrt(2 * F))}
    _L0_attn_in = _L0_attn_setup()

    def _L0_ffn_setup():
        import jax, jax.numpy as jnp
        import numpy as np
        H = 8
        KD = 128
        TOPK = 8
        NUM_KEYS = 32
        N_EXPERTS = NUM_KEYS * NUM_KEYS
        N_DIM = 128
        BN_EPS = 1e-05

        def gelu_new(x):
            c = jnp.sqrt(jnp.asarray(2.0 / jnp.pi, x.dtype))
            return 0.5 * x * (1.0 + jnp.tanh(c * (x + 0.044715 * x * x * x)))
        key = jax.random.key(seed)
        ks = jax.random.split(key, 5)
        b, s = (2, 128)
        x = jax.random.normal(ks[0], (b, s, N_DIM), dtype=jnp.float32)
        w_q = jax.random.normal(ks[1], (N_DIM, 2 * H * KD), dtype=jnp.float32) * 0.02
        bn_gamma = jnp.ones((2 * H * KD,), dtype=jnp.float32)
        bn_beta = jnp.zeros((2 * H * KD,), dtype=jnp.float32)
        keys = jax.random.normal(ks[2], (H, NUM_KEYS, 2, KD), dtype=jnp.float32) * 0.02
        down_embed = jax.random.normal(ks[3], (N_EXPERTS, N_DIM), dtype=jnp.float32) * 0.02
        up_embed = jax.random.normal(ks[4], (N_EXPERTS, N_DIM), dtype=jnp.float32) * 0.02
        return {'x': x, 'w_q': w_q, 'bn_gamma': bn_gamma, 'bn_beta': bn_beta, 'keys': keys, 'down_embed': down_embed, 'up_embed': up_embed}
    _L0_ffn_in = _L0_ffn_setup()
    _d = {'L0_attn_x': _L0_attn_in['x'], 'L0_attn_W_spec': _L0_attn_in['W_spec'], 'L0_attn_W_decay': _L0_attn_in['W_decay'], 'L0_attn_b_decay': _L0_attn_in['b_decay'], 'L0_attn_freqs': _L0_attn_in['freqs'], 'L0_attn_W_out': _L0_attn_in['W_out'], 'L0_ffn_w_q': _L0_ffn_in['w_q'], 'L0_ffn_bn_gamma': _L0_ffn_in['bn_gamma'], 'L0_ffn_bn_beta': _L0_ffn_in['bn_beta'], 'L0_ffn_keys': _L0_ffn_in['keys'], 'L0_ffn_down_embed': _L0_ffn_in['down_embed'], 'L0_ffn_up_embed': _L0_ffn_in['up_embed']}
    _x0 = _d['L0_attn_x']
    _d['L0_attn_x'] = jax.random.normal(jax.random.fold_in(jax.random.key(seed), 1), (8, 512, 128), dtype=_x0.dtype)
    del _x0
    return _d

def reference(L0_attn_x, L0_attn_W_spec, L0_attn_W_decay, L0_attn_b_decay, L0_attn_freqs, L0_attn_W_out, L0_ffn_w_q, L0_ffn_bn_gamma, L0_ffn_bn_beta, L0_ffn_keys, L0_ffn_down_embed, L0_ffn_up_embed):

    def _L0_attn_ref(x, W_spec, W_decay, b_decay, freqs, W_out):
        import jax, jax.numpy as jnp
        import numpy as np
        B, L, D, F = (4, 512, 128, 64)

        def _reference_tuple_inner(x, W_spec, W_decay, b_decay, freqs, W_out):
            Bb, Ll, _ = x.shape
            nf = freqs.shape[0]
            decay = jax.nn.sigmoid(jnp.einsum('bld,df->blf', x, W_decay) + b_decay)
            omega = freqs * 0.1
            rot = jnp.cos(omega) + 1j * jnp.sin(omega)
            spectral = jnp.einsum('bld,df->blf', x, W_spec)
            u = (spectral[..., :nf] + 1j * spectral[..., nf:]).astype(jnp.complex64)
            a = decay.astype(jnp.complex64) * rot

            def step(h, au):
                a_t, u_t = au
                h = a_t * h + u_t
                return (h, h)
            h0 = jnp.zeros((Bb, nf), dtype=jnp.complex64)
            a_t = jnp.transpose(a, (1, 0, 2))
            u_t = jnp.transpose(u, (1, 0, 2))
            h_final, hs = jax.lax.scan(step, h0, (a_t, u_t))
            hs = jnp.transpose(hs, (1, 0, 2))
            y = jnp.concatenate([hs.real, hs.imag], axis=-1)
            out = jnp.einsum('blf,fd->bld', y, W_out)
            return (out, (h_final.real, h_final.imag))
        return _reference_tuple_inner(x, W_spec, W_decay, b_decay, freqs, W_out)[0]

    def _L0_ffn_ref(x, w_q, bn_gamma, bn_beta, keys, down_embed, up_embed):
        import jax, jax.numpy as jnp
        import numpy as np
        H = 8
        KD = 128
        TOPK = 8
        NUM_KEYS = 32
        N_EXPERTS = NUM_KEYS * NUM_KEYS
        N_DIM = 128
        BN_EPS = 1e-05

        def gelu_new(x):
            c = jnp.sqrt(jnp.asarray(2.0 / jnp.pi, x.dtype))
            return 0.5 * x * (1.0 + jnp.tanh(c * (x + 0.044715 * x * x * x)))
        b, n, d = x.shape
        q = jnp.einsum('bnd,de->bne', x, w_q)
        mean = jnp.mean(q, axis=(0, 1))
        var = jnp.var(q, axis=(0, 1))
        q = (q - mean) * jax.lax.rsqrt(var + BN_EPS) * bn_gamma + bn_beta
        q = q.reshape(b, n, 2, H, KD).transpose(2, 0, 1, 3, 4)
        sim = jnp.einsum('pbnhd,hkpd->pbnhk', q, keys)
        sx, ix = jax.lax.top_k(sim[0], TOPK)
        sy, iy = jax.lax.top_k(sim[1], TOPK)
        all_scores = (sx[..., :, None] + sy[..., None, :]).reshape(b, n, H, TOPK * TOPK)
        all_indices = (ix[..., :, None] * NUM_KEYS + iy[..., None, :]).reshape(b, n, H, TOPK * TOPK)
        scores, pk = jax.lax.top_k(all_scores, TOPK)
        indices = jnp.take_along_axis(all_indices, pk, axis=-1)
        wd = down_embed[indices]
        wu = up_embed[indices]
        h = jnp.einsum('bnd,bnhkd->bnhk', x, wd)
        h = gelu_new(h)
        h = jax.nn.softmax(scores, axis=-1) * h
        out = jnp.einsum('bnhk,bnhkd->bnd', h, wu)
        return out
    x = L0_attn_x
    x = x + _L0_attn_ref(_layernorm(x, axis=-1), L0_attn_W_spec, L0_attn_W_decay, L0_attn_b_decay, L0_attn_freqs, L0_attn_W_out)
    x = x + _L0_ffn_ref(_layernorm(x, axis=-1), L0_ffn_w_q, L0_ffn_bn_gamma, L0_ffn_bn_beta, L0_ffn_keys, L0_ffn_down_embed, L0_ffn_up_embed)
    return x

_drawn_inputs = setup_inputs


def setup_inputs(seed=0):
    import zlib

    import numpy as np

    out = dict(_drawn_inputs(seed))
    spreads = {'L0_ffn_bn_gamma': (1.0, 0.6), 'L0_ffn_bn_beta': (0.0, 0.8)}
    factors = {'L0_attn_b_decay': 8.0,
     'L0_ffn_w_q': 8.0,
     'L0_ffn_keys': 8.0,
     'L0_ffn_down_embed': 8.0,
     'L0_ffn_up_embed': 8.0}
    for name, (base, spread) in spreads.items():
        noise = np.random.default_rng([zlib.crc32(name.encode()), seed]).standard_normal(out[name].shape)
        drawn = base * np.exp(spread * noise) if base else spread * noise
        out[name] = jnp.asarray(drawn.astype(out[name].dtype))
    for name, factor in factors.items():
        out[name] = (out[name] * factor).astype(out[name].dtype)
    return out
```

```python
from contextlib import ExitStack
import math

import concourse.bass as bass
from concourse import mybir

ALU = mybir.AluOpType
ACT = mybir.ActivationFunctionType
AX = mybir.AxisListType
F32 = mybir.dt.float32
F16 = mybir.dt.float16
U32 = mybir.dt.uint32

P = 128
D = 128
SEQ = 512
GROUPS = 8
TILES = SEQ // P
NTOK = GROUPS * SEQ
F = 64
H = 8
KD = 128
NK = 32
TOP = 8
HF = 2 * H
LO = 8
CH = TILES * H
COLS = SEQ // 2
EPS = 1e-5
ROUND = 1.5 * 2.0 ** 23
COARSE = 1.5 * 2.0 ** 10
WSCALE = 2.0 ** 14
PAIRS = [(a, b) for a in range(TOP) for b in range(TOP) if (a + 1) * (b + 1) <= TOP]
NP = len(PAIRS)
AROWS = ((0, 1, 8), (1, 2, 4), (2, 4, 2), (4, 8, 1))


def wait(eng, sem, value):
    if isinstance(value, int) and value <= 0:
        return
    eng.wait_ge(sem, value)


class Chain:

    def __init__(self, eng, sem):
        self.eng, self.sem, self.n = eng, sem, 0

    def done(self, ins):
        ins.then_inc(self.sem, 1)
        self.n += 1
        return self.n

    def wait(self, n):
        self.eng.wait_ge(self.sem, n)

    def restart(self):
        if self.n:
            self.wait(self.n)
            self.eng.sem_clear(self.sem)
        self.n = 0


def touch(dve, sem, value, cell):
    wait(dve, sem, value)
    dve.memset(cell, 0.0)


def steps(eng, nstages, body):
    first = nstages - 1 + (nstages - 1) % 2
    last = GROUPS - GROUPS % 2
    for s in range(first):
        body(s, s % 2)
    with eng.Fori(first // 2, last // 2) as i:
        for q in range(2):
            body(i * 2 + q, q)
    for s in range(last, GROUPS + nstages - 1):
        body(s, s % 2)


def active(s, lag):
    return not isinstance(s, int) or 0 <= s - lag < GROUPS


def build(nc, x, w_spec, w_decay, b_decay, freqs, w_out, w_q, bn_gamma, bn_beta, keys, down, up, out):
    with ExitStack() as whole:
        def sb(name, shape, dt=F32, ctx=whole):
            return ctx.enter_context(nc.sbuf_tensor(name, shape, dt))

        def sem(name):
            return whole.enter_context(nc.semaphore(name))

        banks = [whole.enter_context(nc.psum_tensor(f"bank{i}", [P, 512], F32)) for i in range(8)]

        x_sb = sb("x_sb", [P, NTOK])
        xn2T_all = sb("xn2T_all", [P, NTOK])
        ident = sb("ident", [P, P])
        ones = sb("ones", [P, P])
        eps_row = sb("eps_row", [P, TILES])
        downT = sb("downT", [P, LO, P])
        up_sb = sb("up_sb", [P, LO, D])
        fold_M = sb("fold_M", [P, HF * NK])
        fold_b = sb("fold_b", [1, HF * NK])
        idle = sb("idle", [1, 2 * (TILES + 1)])
        half_pow = sb("half_pow", [P, 16])

        xr = x.rearrange("b (c p) d -> p (b c) d", p=P)

        with ExitStack() as ctx:
            def a(name, shape, dt=F32):
                return sb(name, shape, dt, ctx)

            wq_sb = a("wq_sb", [P, HF * KD])
            keys_sb = a("keys_sb", [P, 2, 2, KD])
            down_sb = a("down_sb", [P, LO, D])
            gb_sb = a("gb_sb", [2 * HF, KD])
            wspec = a("wspec", [P, 2 * F])
            wswap = a("wswap", [P, 2 * F])
            wdec = a("wdec", [P, 2 * F])
            wout = a("wout", [P, D])
            woutsw = a("woutsw", [P, D])
            bdec = a("bdec", [P, 1])
            freq = a("freq", [P, 1])
            rates = a("rates", [P, 5])
            sgn = a("sgn", [P, 1])
            pos_t = a("pos_t", [P, SEQ])
            ph = a("ph", [P, 5, SEQ])
            cosT = a("cosT", [P, SEQ])
            sinT = a("sinT", [P, SEQ])
            st1 = a("st1", [P, 2, TILES, 6])
            mv1 = a("mv1", [P, 2, TILES, 2])
            rs1 = a("rs1", [P, 2, TILES])
            xn1 = a("xn1", [P, 2, SEQ])
            xn1T = a("xn1T", [P, 2, SEQ])
            decay = a("decay", [P, 2, SEQ])
            rot1 = a("rot1", [P, 2, SEQ])
            rot2 = a("rot2", [P, 2, SEQ])
            pin = a("pin", [P, 2, SEQ])
            state = a("state", [P, 2, SEQ])
            gcos = a("gcos", [P, 2, SEQ])
            gsin = a("gsin", [P, 2, SEQ])
            st2 = a("st2", [P, 2, TILES, 6])
            mv2 = a("mv2", [P, 2, TILES, 2])
            ve1 = a("ve1", [P, 2, TILES])
            ve2 = a("ve2", [P, 2, TILES])
            rs2 = a("rs2", [P, 2, TILES])
            xn2 = a("xn2", [P, 2, TILES, D + 1])
            zeros = a("zeros", [P, D + 1])
            wqT = a("wqT", [P, HF, P])
            keysT = a("keysT", [P, HF, NK])
            gbT = a("gbT", [P, 2 * HF])
            gram = a("gram", [P, P + 1])
            prod = a("prod", [P, HF * KD])
            stat = a("stat", [P, 6, HF])
            normA = a("normA", [P, HF])
            normB = a("normB", [P, HF])
            keysA = a("keysA", [P, HF, NK])

            x_first, x_rest, w_in, w_late = sem("x_first"), sem("x_rest"), sem("w_in"), sem("w_late")
            consts, tables, table_step, sines = sem("consts"), sem("tables"), sem("table_step"), sem("sines")
            aggr1, rstd1, xn1_done = sem("aggr1"), sem("rstd1"), sem("xn1_done")
            xn1_psum, xn1T_done, spec_mm, decay_mm = sem("xn1_psum"), sem("xn1T_done"), sem("spec_mm"), sem("decay_mm")
            decay_done, rotated, pin_done, scanned = sem("decay_done"), sem("rotated"), sem("pin_done"), sem("scanned")
            rot_out, out_mm, x1_done = sem("rot_out"), sem("out_mm"), sem("x1_done")
            aggr2, rstd2, xn2_done = sem("aggr2"), sem("rstd2"), sem("xn2_done")
            xn2_psum, xn2T_done, gram_done = sem("xn2_psum"), sem("xn2T_done"), sem("gram_done")
            pool_chain, dve_chain = sem("pool_chain"), sem("dve_chain")
            late_mm, late_ev = sem("late_mm"), sem("late_ev")

            tp1, spec_u, spec_s, dec_p, out_p, tp2, gram_p, late_p = banks

            with nc.Block() as block:
                @block.sync
                def _(sp):
                    sp.dma_start(x_sb[:, 0:2 * SEQ].rearrange("p (t d) -> p t d", d=D), xr[:, 0:2 * TILES, :]).then_inc(x_first, 16)
                    for dst, src in ((freq[0:F, :], freqs.rearrange("(f a) -> f a", a=1)),
                                     (freq[F:P, :], freqs.rearrange("(f a) -> f a", a=1)),
                                     (bdec[0:F, :], b_decay.rearrange("(f a) -> f a", a=1)),
                                     (bdec[F:P, :], b_decay.rearrange("(f a) -> f a", a=1)),
                                     (wspec[:, :], w_spec), (wswap[:, 0:F], w_spec[:, F:2 * F]),
                                     (wswap[:, F:2 * F], w_spec[:, 0:F]), (wdec[:, 0:F], w_decay),
                                     (wdec[:, F:2 * F], w_decay), (wout[:, :], w_out),
                                     (woutsw[0:F, :], w_out[F:2 * F, :]), (woutsw[F:P, :], w_out[0:F, :])):
                        sp.dma_start(dst, src).then_inc(w_in, 16)
                    sp.dma_start(x_sb[:, 2 * SEQ:].rearrange("p (t d) -> p t d", d=D), xr[:, 2 * TILES:, :]).then_inc(x_rest, 16)
                    for dst, src in ((gb_sb[0:HF, :], bn_gamma.rearrange("(j k) -> j k", k=KD)),
                                     (gb_sb[HF:2 * HF, :], bn_beta.rearrange("(j k) -> j k", k=KD)),
                                     (keys_sb[:, :, :, :], keys.rearrange("(a h) k p d -> (h k) a p d", a=2)),
                                     (down_sb[:, :, :], down.rearrange("(c l) d -> c l d", l=LO)),
                                     (up_sb[:, :, :], up.rearrange("(c l) d -> c l d", l=LO)),
                                     (wq_sb[:, :], w_q)):
                        sp.dma_start(dst, src).then_inc(w_late, 16)

                W_IN, W_LATE = 16 * 12, 16 * 6

                @block.gpsimd
                def _(pool):
                    pool.memset(half_pow[:, :], -0.5)
                    pool.memset(eps_row[:, :], EPS)
                    pool.iota(pos_t[:, :], pattern=[[1, SEQ]], base=0, channel_multiplier=0,
                              allow_small_or_imprecise_dtypes=True).then_inc(tables, 1)
                    pool.memset(zeros[:, :], 0.0)
                    pool.memset(ones[:, :], 1.0)
                    pool.memset(xn2[:, :, :, D:D + 1], 1.0).then_inc(consts, 1)
                    pool.wait_ge(consts, 1)
                    pool.affine_select(out=ident[:, :], in_=zeros[:, 0:P], compare_op=ALU.not_equal, fill=1.0,
                                       base=0, pattern=[[-1, P]], channel_multiplier=1).then_inc(consts, 1)

                    def body(s, q):
                        g, g1, g2, r = s, s - 1, s - 2, 1 - q
                        if active(s, 0):
                            wait(pool, aggr1, g + 1)
                            chain.wait(chain.done(pool.tensor_tensor(ve1[:, q, :], mv1[:, q, :, 1], eps_row[:, :], ALU.add)))
                            pool.tensor_tensor(rs1[:, q, :], ve1[:, q, :], half_pow[:, 0:TILES], ALU.pow).then_inc(rstd1, 1)
                        if active(s, 1):
                            wait(pool, rotated, g1 + 1)
                            wait(pool, scanned, g1 - 1)
                            pool.tensor_tensor(pin[:, r, :], rot1[:, r, :], rot2[:, r, :], ALU.add).then_inc(pin_done, 1)
                        if active(s, 2):
                            wait(pool, aggr2, g2 + 1)
                            chain.wait(chain.done(pool.tensor_tensor(ve2[:, q, :], mv2[:, q, :, 1], eps_row[:, :], ALU.add)))
                            pool.tensor_tensor(rs2[:, q, :], ve2[:, q, :], half_pow[:, 0:TILES], ALU.pow).then_inc(rstd2, 1)
                        if active(s, 1):
                            wait(pool, scanned, g1 + 1)
                            wait(pool, out_mm, g1 - 1)
                            pool.tensor_tensor(gcos[:, r, :], state[:, r, :], cosT[:, :], ALU.mult)
                            pool.tensor_tensor(gsin[:, r, :], state[:, r, :], sinT[:, :], ALU.mult).then_inc(rot_out, 1)
                        chain.restart()

                    chain = Chain(pool, pool_chain)
                    pool.wait_ge(sines, 2)
                    steps(pool, 3, body)

                @block.scalar
                def _(act):
                    act.wait_ge(table_step, 16)
                    act.activation(cosT[:, :], ph[:, 1, :], ACT.Sin, scale=6.2831850).then_inc(sines, 1)
                    act.activation(sinT[:, :], ph[:, 2, :], ACT.Sin, scale=sgn[:, 0:1]).then_inc(sines, 1)

                    def body(s, q):
                        g, g2 = s, s - 2
                        if active(s, 0):
                            wait(act, xn1_psum, g + 1)
                            act.copy(xn1T[:, q, :], tp1[:, :]).then_inc(xn1T_done, 1)
                        if active(s, 2):
                            wait(act, xn2_psum, g2 + 1)
                            act.copy(xn2T_all[:, bass.ds(g2 * SEQ, SEQ)], tp2[:, :]).then_inc(xn2T_done, 1)
                        if active(s, 0):
                            wait(act, decay_mm, g + 1)
                            wait(act, scanned, g - 1)
                            act.activation(decay[:, q, :], dec_p[:, :], ACT.Sigmoid, bias=bdec[:, 0:1]).then_inc(decay_done, 1)
                        if isinstance(s, int) and s == 1:
                            for n in range(8):
                                act.wait_ge(late_mm, n + 1)
                                if n < 4:
                                    dst, src = wqT[:, 4 * n:4 * n + 4, :], late_p[:, :].rearrange("p (j d) -> p j d", d=P)
                                elif n < 6:
                                    dst = keysT[:, (n - 4) * H:(n - 3) * H, :]
                                    src = late_p[:, 0:H * NK].rearrange("p (h k) -> p h k", k=NK)
                                else:
                                    dst, src = downT[:, 4 * (n - 6):4 * (n - 5), :], late_p[:, :].rearrange("p (j d) -> p j d", d=P)
                                act.copy(dst, src).then_inc(late_ev, 1)
                            act.wait_ge(late_mm, 9)
                            act.copy(gbT[:, :], late_p[:, 0:2 * HF]).then_inc(late_ev, 1)

                    steps(act, 3, body)

                @block.vector
                def _(dve):
                    done = [0]

                    def then(ins):
                        ins.then_inc(table_step, 1)
                        done[0] += 1
                        dve.wait_ge(table_step, done[0])

                    dve.memset(sgn[0:F, :], 6.2831850)
                    dve.memset(sgn[F:P, :], -6.2831850)
                    dve.wait_ge(w_in, W_IN)
                    dve.wait_ge(tables, 1)
                    then(dve.tensor_scalar(rates[:, 0:1], freq[:, :], 0.1, None, ALU.mult))
                    then(dve.tensor_scalar(rates[:, 1:2], rates[:, 0:1], 1.0 / (2.0 * math.pi), None, ALU.mult))
                    then(dve.tensor_scalar(rates[:, 2:3], rates[:, 1:2], COARSE, None, ALU.add))
                    then(dve.tensor_scalar(rates[:, 3:4], rates[:, 2:3], COARSE, None, ALU.subtract))
                    then(dve.tensor_tensor(rates[:, 4:5], rates[:, 1:2], rates[:, 3:4], ALU.subtract))
                    then(dve.tensor_scalar(ph[:, 0, :], pos_t[:, :], rates[:, 3:4], None, ALU.mult))
                    then(dve.tensor_scalar(ph[:, 3, :], ph[:, 0, :], ROUND, None, ALU.add))
                    then(dve.tensor_scalar(ph[:, 4, :], ph[:, 3, :], ROUND, None, ALU.subtract))
                    then(dve.tensor_tensor(ph[:, 3, :], ph[:, 0, :], ph[:, 4, :], ALU.subtract))
                    then(dve.scalar_tensor_tensor(out=ph[:, 0, :], in0=pos_t[:, :], scalar=rates[:, 4:5], in1=ph[:, 3, :],
                                                  op0=ALU.mult, op1=ALU.add))
                    for to, shift in ((2, 0.0), (1, 0.25)):
                        then(dve.tensor_scalar(ph[:, 3, :], ph[:, 0, :], shift, ROUND, ALU.add, ALU.add))
                        then(dve.tensor_scalar(ph[:, 4, :], ph[:, 3, :], ROUND, None, ALU.subtract))
                        then(dve.scalar_tensor_tensor(out=ph[:, to, :], in0=ph[:, 0, :], scalar=shift, in1=ph[:, 4, :],
                                                      op0=ALU.add, op1=ALU.subtract))

                    def body(s, q):
                        g, g1, g2, r = s, s - 1, s - 2, 1 - q

                        def tile(group, c):
                            return x_sb[:, bass.ds(group * SEQ + c * P, P)]

                        if active(s, 0):
                            if isinstance(s, int):
                                dve.wait_ge(x_first, 16)
                            else:
                                dve.wait_ge(x_rest, 16)
                            for c in range(TILES):
                                ins = dve.bn_stats(st1[:, q, c, :], tile(g, c))
                            stats1 = chain.done(ins)
                        if active(s, 1):
                            if isinstance(s, int) and s == 1:
                                dve.wait_ge(sines, 2)
                            wait(dve, spec_mm, g1 + 1)
                            wait(dve, pin_done, g1 - 1)
                            dve.tensor_tensor(rot1[:, r, :], spec_u[:, :], cosT[:, :], ALU.mult)
                            dve.tensor_tensor(rot2[:, r, :], spec_s[:, :], sinT[:, :], ALU.mult).then_inc(rotated, 1)
                        if active(s, 0):
                            chain.wait(stats1)
                            for c in range(TILES):
                                ins = dve.bn_aggr(mv1[:, q, c, :], st1[:, q, c, :])
                            ins.then_inc(aggr1, 1)
                        if active(s, 2):
                            wait(dve, out_mm, g2 + 1)
                            dve.tensor_tensor(x_sb[:, bass.ds(g2 * SEQ, SEQ)], out_p[:, :],
                                              x_sb[:, bass.ds(g2 * SEQ, SEQ)], ALU.add).then_inc(x1_done, 1)
                            touch(dve, x1_done, g2 + 1, idle[:, 2 * TILES + q:2 * TILES + q + 1])
                            for c in range(TILES):
                                ins = dve.bn_stats(st2[:, q, c, :], tile(g2, c))
                            chain.wait(chain.done(ins))
                            for c in range(TILES):
                                ins = dve.bn_aggr(mv2[:, q, c, :], st2[:, q, c, :])
                            ins.then_inc(aggr2, 1)
                        if active(s, 0):
                            wait(dve, rstd1, g + 1)
                            wait(dve, xn1_psum, g - 1)
                            for c in range(TILES):
                                ins = dve.tensor_scalar(xn1[:, q, c * P:(c + 1) * P], tile(g, c), mv1[:, q, c, 0:1],
                                                        rs1[:, q, c:c + 1], ALU.subtract, ALU.mult)
                            ins.then_inc(xn1_done, 1)
                        if active(s, 1):
                            wait(dve, pin_done, g1 + 1)
                            wait(dve, decay_done, g1 + 1)
                            wait(dve, rot_out, g1 - 1)
                            dve.tensor_tensor_scan(out=state[:, r, :], data0=decay[:, r, :], data1=pin[:, r, :],
                                                   initial=0.0, op0=ALU.mult, op1=ALU.add).then_inc(scanned, 1)
                        if active(s, 2):
                            wait(dve, rstd2, g2 + 1)
                            for c in range(TILES):
                                ins = dve.tensor_scalar(xn2[:, q, c, 0:D], tile(g2, c), mv2[:, q, c, 0:1],
                                                        rs2[:, q, c:c + 1], ALU.subtract, ALU.mult)
                            ins.then_inc(xn2_done, 1)
                        chain.restart()

                    chain = Chain(dve, dve_chain)
                    steps(dve, 3, body)

                @block.tensor
                def _(pe):
                    pe.wait_ge(consts, 2)
                    pe.matmul(gram_p[:, 0:P + 1], zeros[:, 0:P], zeros[:, :], start=True, stop=False)

                    def late_transposes():
                        pe.wait_ge(w_late, W_LATE)
                        for n in range(9):
                            if n:
                                pe.wait_ge(late_ev, n)
                            if n < 4:
                                for j in range(4):
                                    m = pe.transpose(late_p[:, j * P:(j + 1) * P], wq_sb[:, (4 * n + j) * KD:(4 * n + j + 1) * KD], ident[:, :])
                            elif n < 6:
                                for b in range(2):
                                    m = pe.transpose(late_p[:, b * P:(b + 1) * P], keys_sb[:, b, n - 4, :], ident[:, :])
                            elif n < 8:
                                for j in range(4):
                                    m = pe.transpose(late_p[:, j * P:(j + 1) * P], down_sb[:, 4 * (n - 6) + j, :], ident[:, :])
                            else:
                                m = pe.transpose(late_p[:, 0:2 * HF], gb_sb[:, :], ident[0:2 * HF, 0:2 * HF])
                            m.then_inc(late_mm, 1)

                    def body(s, q):
                        g, g1, g2, r = s, s - 1, s - 2, 1 - q
                        if active(s, 0):
                            wait(pe, xn1_done, g + 1)
                            wait(pe, xn1T_done, g)
                            for c in range(TILES):
                                m = pe.transpose(tp1[:, c * P:(c + 1) * P], xn1[:, q, c * P:(c + 1) * P], ident[:, :])
                            m.then_inc(xn1_psum, 1)
                            if isinstance(s, int) and s == 0:
                                pe.wait_ge(w_in, W_IN)
                            wait(pe, xn1T_done, g + 1)
                            wait(pe, decay_done, g)
                            pe.matmul(dec_p[:, :], wdec[:, :], xn1T[:, q, :], start=True, stop=True).then_inc(decay_mm, 1)
                            wait(pe, rotated, g)
                            pe.matmul(spec_u[:, :], wspec[:, :], xn1T[:, q, :], start=True, stop=True)
                            pe.matmul(spec_s[:, :], wswap[:, :], xn1T[:, q, :], start=True, stop=True).then_inc(spec_mm, 1)
                        if isinstance(s, int) and s == 1:
                            late_transposes()
                        if active(s, 1):
                            wait(pe, rot_out, g1 + 1)
                            wait(pe, x1_done, g1)
                            for c in range(TILES):
                                pe.matmul(out_p[:, c * D:(c + 1) * D], gcos[:, r, c * P:(c + 1) * P], wout[:, :], start=True, stop=False)
                                m = pe.matmul(out_p[:, c * D:(c + 1) * D], gsin[:, r, c * P:(c + 1) * P], woutsw[:, :], start=False, stop=True)
                            m.then_inc(out_mm, 1)
                        if active(s, 2):
                            wait(pe, xn2_done, g2 + 1)
                            for c in range(TILES):
                                pe.matmul(gram_p[:, 0:P + 1], xn2[:, q, c, 0:D], xn2[:, q, c, :], start=False, stop=False)
                            wait(pe, xn2T_done, g2)
                            for c in range(TILES):
                                m = pe.transpose(tp2[:, c * P:(c + 1) * P], xn2[:, q, c, 0:D], ident[:, :])
                            m.then_inc(xn2_psum, 1)

                    steps(pe, 3, body)
                    pe.matmul(gram_p[:, 0:P + 1], zeros[:, 0:P], zeros[:, :], start=False, stop=True).then_inc(gram_done, 1)

            fold = sem("fold")
            fold_t, fold_e, fold_m, fold_rs, fold_ev = sem("fold_t"), sem("fold_e"), sem("fold_m"), sem("fold_rs"), sem("fold_ev")
            with nc.Block() as block:
                @block.vector
                def _(dve):
                    done = [0]

                    def then(ins):
                        ins.then_inc(fold, 1)
                        done[0] += 1
                        dve.wait_ge(fold, done[0])

                    dve.wait_ge(gram_done, 1)
                    then(dve.tensor_scalar(gram[:, :], gram_p[:, 0:P + 1], 1.0 / NTOK, None, ALU.mult))
                    for n in range(4):
                        dve.wait_ge(fold_t, n + 1)
                        ins = dve.tensor_tensor(prod[:, n * 512:(n + 1) * 512], banks[n][:, :], wq_sb[:, n * 512:(n + 1) * 512], ALU.mult)
                        ins.then_inc(fold, 1)
                        done[0] += 1
                    dve.wait_ge(fold_e, 1)
                    sq, mean = banks[4][:, 0:HF], banks[4][:, HF:2 * HF]
                    then(dve.tensor_copy(stat[:, 0, :], mean))
                    then(dve.tensor_tensor(stat[:, 1, :], stat[:, 0, :], stat[:, 0, :], ALU.mult))
                    then(dve.tensor_tensor(stat[:, 2, :], sq, stat[:, 1, :], ALU.subtract))
                    then(dve.tensor_scalar(stat[:, 3, :], stat[:, 2, :], 0.0, EPS, ALU.max, ALU.add))
                    dve.wait_ge(fold_rs, 1)
                    then(dve.tensor_tensor(normA[:, :], stat[:, 4, :], gbT[:, 0:HF], ALU.mult))
                    then(dve.tensor_tensor(stat[:, 5, :], stat[:, 0, :], normA[:, :], ALU.mult))
                    dve.tensor_tensor(normB[:, :], gbT[:, HF:2 * HF], stat[:, 5, :], ALU.subtract).then_inc(fold, 1)
                    dve.tensor_tensor(keysA[:, :, :], keysT[:, :, :], normA[:, :].unsqueeze(2).to_broadcast([P, HF, NK]),
                                      ALU.mult).then_inc(fold, 1)

                @block.gpsimd
                def _(pool):
                    pool.wait_ge(fold, 9)
                    pool.tensor_tensor(stat[:, 4, :], stat[:, 3, :], half_pow[:, :], ALU.pow).then_inc(fold_rs, 1)

                @block.tensor
                def _(pe):
                    pe.wait_ge(fold, 1)
                    for n in range(4):
                        pe.matmul(banks[n][:, :], gram[:, 0:P], wq_sb[:, n * 512:(n + 1) * 512], start=True, stop=True).then_inc(fold_t, 1)
                    for j in range(HF):
                        pe.matmul(banks[4][:, HF + j:HF + j + 1], wq_sb[:, j * KD:(j + 1) * KD], gram[:, P:P + 1], start=True, stop=True)
                    pe.wait_ge(fold, 5)
                    for j in range(HF):
                        m = pe.matmul(banks[4][:, j:j + 1], prod[:, j * KD:(j + 1) * KD], ones[:, 0:1], start=True, stop=True)
                    m.then_inc(fold_e, 1)
                    pe.wait_ge(fold, 13)
                    for j in range(HF):
                        pe.matmul(banks[5][:, j * NK:(j + 1) * NK], wqT[:, j, :], keysA[:, j, :], start=True, stop=True)
                        m = pe.matmul(banks[6][0:1, j * NK:(j + 1) * NK], normB[:, j:j + 1], keysT[:, j, :], start=True, stop=True)
                    m.then_inc(fold_m, 1)

                @block.scalar
                def _(act):
                    act.wait_ge(fold_m, 1)
                    act.copy(fold_M[:, :], banks[5][:, :])
                    act.copy(fold_b[:, :], banks[6][0:1, :]).then_inc(fold_ev, 1)

        with ExitStack() as ctx:
            def a(name, shape, dt=F32):
                return sb(name, shape, dt, ctx)

            xs = a("xs", [P, 2, SEQ])
            sim = a("sim", [P, TILES, HF, NK])
            best = a("best", [P, 2, CH, TOP])
            bidx = a("bidx", [P, 2, CH, TOP], U32)
            idx = a("idx", [P, 2, 2, CH, TOP])
            cand = a("cand", [P, CH, NP])
            ecand = a("ecand", [P, CH, NP])
            top = a("top", [P, CH, TOP])
            posu = a("posu", [P, 2, CH, TOP], U32)
            gap = a("gap", [P, 2, CH, TOP])
            ex = a("ex", [P, CH, TOP])
            esum = a("esum", [P, CH])
            einv = a("einv", [P, CH])
            wslot = a("wslot", [P, CH, TOP])
            eslot = a("eslot", [P, CH, TOP])
            eq = a("eq", [P, CH, TOP])
            sl = a("sl", [P, 4, COLS])
            rowid = a("rowid", [P, COLS], F16)
            colid = a("colid", [P, COLS], F16)
            whi = a("whi", [P, COLS], F16)
            wlo = a("wlo", [P, COLS], F16)
            half_off = a("half_off", [P, 1])
            X = a("X", [P, P, COLS], F16)
            Yhi = a("Yhi", [P, 2 * LO, COLS], F16)
            Ylo = a("Ylo", [P, 2 * LO, COLS], F16)
            act_g = a("act_g", [P, LO, SEQ])
            wsb = a("wsb", [P, LO, SEQ])
            ob = a("ob", [P, 2, SEQ])

            simp, gp, wp, slot_p, up_p = banks[0:2], banks[2:4], banks[4:6], banks[6], banks[7]
            xs_in = [sem("xs_in0"), sem("xs_in1")]
            out_sent = [sem("out_sent0"), sem("out_sent1")]
            sim_mm = [sem(f"sim_mm{c}") for c in range(TILES)]
            sim_ev = [sem(f"sim_ev{c}") for c in range(TILES)]
            g_mm, g_ev, w_mm, w_ev, wg_done, up_mm = sem("g_mm"), sem("g_ev"), sem("w_mm"), sem("w_ev"), sem("wg_done"), sem("up_mm")
            axis_top, gap_done, exp_done, w_done = sem("axis_top"), sem("gap_done"), sem("exp_done"), sem("w_done")
            e_done, slots_mm = sem("e_done"), sem("slots_mm")
            built, fin = sem("built"), sem("fin")
            NB = 8
            TB = COLS // NB
            half_ready = sem("half_ready")

            with nc.Block() as block:
                @block.sync
                def _(sp):
                    def body(s, q):
                        if active(s, 0):
                            wait(sp, sim_mm[TILES - 1], s - 1)
                            sp.dma_start(xs[:, q, :], xn2T_all[:, bass.ds(s * SEQ, SEQ)]).then_inc(xs_in[q], 16)
                        if active(s, 2):
                            wait(sp, fin, s - 2 + 1)
                            sp.dma_start(out[bass.ds(s - 2, 1)].rearrange("b (c p) d -> p (b c) d", p=P),
                                         ob[:, q, :].rearrange("p (c d) -> p c d", d=D)).then_inc(out_sent[q], 16)

                    steps(sp, 3, body)
                    for q in range(2):
                        sp.wait_ge(out_sent[q], 16 * GROUPS // 2)

                @block.tensor
                def _(pe):
                    pe.wait_ge(fold_ev, 1)

                    def body(s, q):
                        g, g1, g2 = s, s - 1, s - 2
                        if active(s, 0):
                            pe.wait_ge(xs_in[q], xs_count(s, q))
                            for c in range(TILES):
                                wait(pe, sim_ev[(c + 2) % TILES], g + 1 if c >= 2 else g)
                                pe.matmul(simp[c % 2][:, :], xs[:, q, c * P:(c + 1) * P], fold_M[:, :], start=True, stop=False)
                                pe.matmul(simp[c % 2][:, :], ones[0:1, :], fold_b[:, :], start=False, stop=True).then_inc(sim_mm[c], 1)
                        if active(s, 2):
                            for l in range(LO):
                                wait(pe, g_ev, g2 * LO + max(l - 1, 0))
                                pe.matmul(gp[l % 2][:, :], downT[:, l, :], xn2T_all[:, bass.ds(g2 * SEQ, SEQ)],
                                          start=True, stop=True).then_inc(g_mm, 1)
                            wait(pe, built, g2 + 1)
                            for b in range(NB):
                                wait(pe, w_ev, g2 * NB + max(b - 1, 0))
                                for t in range(b * TB, (b + 1) * TB):
                                    o = wp[b % 2][:, (t % TB) * 2 * LO:(t % TB + 1) * 2 * LO]
                                    pe.matmul(o, X[:, :, t], Yhi[:, :, t], start=True, stop=False)
                                    m = pe.matmul(o, X[:, :, t], Ylo[:, :, t], start=False, stop=True)
                                m.then_inc(w_mm, 1)
                            wait(pe, fin, g2)
                            for c in range(TILES):
                                wait(pe, wg_done, g2 * TILES + c + 1)
                                for l in range(LO):
                                    m = pe.matmul(up_p[:, c * D:(c + 1) * D], wsb[:, l, c * P:(c + 1) * P], up_sb[:, l, :],
                                                  start=(l == 0), stop=(l == LO - 1))
                            m.then_inc(up_mm, 1)
                        if active(s, 1):
                            wait(pe, e_done, g1 + 1)
                            wait(pe, w_done, g1 + 1)
                            wait(pe, built, g1)
                            for m2 in range(2):
                                for k, src in enumerate((eslot, wslot)):
                                    m = pe.transpose(slot_p[:, (2 * k + m2) * P:(2 * k + m2 + 1) * P],
                                                     src[:, 2 * m2 * H:2 * (m2 + 1) * H, :].rearrange("p c k -> p (c k)"), ident[:, :])
                            m.then_inc(slots_mm, 1)

                    def xs_count(s, q):
                        return (s - q) * 8 + 16

                    steps(pe, 3, body)

                @block.scalar
                def _(act):
                    def body(s, q):
                        g, g2 = s, s - 2
                        if active(s, 0):
                            for c in range(TILES):
                                wait(act, sim_mm[c], g + 1)
                                wait(act, axis_top, g)
                                act.copy(sim[:, c, :, :], simp[c % 2][:, :].rearrange("p (j k) -> p j k", k=NK)).then_inc(sim_ev[c], 1)
                        if active(s, 2):
                            wait(act, wg_done, g2 * TILES)
                            for l in range(LO):
                                wait(act, g_mm, g2 * LO + l + 1)
                                act.activation(act_g[:, l, :], gp[l % 2][:, :], ACT.Gelu_apprx_tanh).then_inc(g_ev, 1)
                            wait(act, up_mm, g2)
                            for b in range(NB):
                                wait(act, w_mm, g2 * NB + b + 1)
                                t0 = (b * TB) % P
                                m2 = b * TB // P
                                dst = wsb[:, :, :].rearrange("p l (m r t) -> p m t r l", m=2, r=2)[:, m2, t0:t0 + TB, :, :]
                                act.copy(dst, wp[b % 2][:, :].rearrange("p (t r l) -> p t r l", r=2, l=LO)).then_inc(w_ev, 1)
                        if active(s, 0):
                            wait(act, gap_done, g + 1)
                            wait(act, w_done, g)
                            act.activation(ex[:, :, :], gap[:, q, :, :], ACT.Exp).then_inc(exp_done, 1)

                    steps(act, 3, body)

                @block.gpsimd
                def _(pool):
                    pool.memset(half_off[0:64, :], 0.0)
                    pool.memset(half_off[64:P, :], float(LO)).then_inc(half_ready, 1)
                    pool.wait_ge(half_ready, 1)

                    def body(s, q):
                        g1, g2, r = s - 1, s - 2, 1 - q
                        if active(s, 1):
                            wait(pool, gap_done, g1 + 1)
                            wait(pool, slots_mm, g1)
                            k = 0
                            for a0, a1, nb in AROWS:
                                n = (a1 - a0) * nb
                                o = ecand[:, :, k:k + n].rearrange("p c (a b) -> p c a b", b=nb)
                                ia = idx[:, r, 0, :, a0:a1].unsqueeze(3).to_broadcast([P, CH, a1 - a0, nb])
                                ib = idx[:, r, 1, :, 0:nb].unsqueeze(2).to_broadcast([P, CH, a1 - a0, nb])
                                ins = pool.tensor_tensor(o, ia, ib, ALU.add)
                                k += n
                            pairs = chain.done(ins)
                            chain.wait(pairs)
                            for c, (pa, pb) in enumerate(PAIRS):
                                k0 = (pa + 1) * (pb + 1) - 1
                                n = TOP - k0
                                e = eq[:, :, k0:]
                                chain.wait(chain.done(pool.tensor_scalar(e, posu[:, r, :, k0:], float(c), None, ALU.is_equal)))
                                src = ecand[:, :, c:c + 1].to_broadcast([P, CH, n])
                                dst = eslot[:, :, :] if c == 0 else e
                                chain.wait(chain.done(pool.tensor_tensor(dst, e, src, ALU.mult)))
                                if c:
                                    ins = pool.tensor_tensor(eslot[:, :, k0:], eslot[:, :, k0:], e, ALU.add)
                                    if c == NP - 1:
                                        ins.then_inc(e_done, 1)
                                    else:
                                        chain.wait(chain.done(ins))
                            chain.restart()
                        if active(s, 2):
                            wait(pool, g_ev, (g2 + 1) * LO)
                            for c in range(TILES):
                                wait(pool, w_ev, g2 * NB + NB // 2 * (c // 2 + 1))
                                w = wsb[:, :, c * P:(c + 1) * P]
                                pool.tensor_tensor(w, w, act_g[:, :, c * P:(c + 1) * P], ALU.mult).then_inc(wg_done, 1)

                    chain = Chain(pool, pool_chain)
                    steps(pool, 3, body)

                @block.vector
                def _(dve):
                    dve.wait_ge(half_ready, 1)
                    chain = Chain(dve, dve_chain)

                    def body(s, q):
                        g, g1, g2, r = s, s - 1, s - 2, 1 - q
                        if active(s, 1):
                            wait(dve, exp_done, g1 + 1)
                            chain.wait(chain.done(dve.tensor_reduce(esum[:, :], ex[:, :, :], AX.X, ALU.add)))
                            chain.wait(chain.done(dve.reciprocal(einv[:, :], esum[:, :])))
                            wait(dve, slots_mm, g1)
                            dve.scalar_tensor_tensor(out=wslot[:, :, :], in0=ex[:, :, :], scalar=WSCALE,
                                                     in1=einv[:, :].unsqueeze(2).to_broadcast([P, CH, TOP]),
                                                     op0=ALU.mult, op1=ALU.mult).then_inc(w_done, 1)
                        if active(s, 2):
                            E_, W_ = slot_p[:, 0:COLS], slot_p[:, COLS:2 * COLS]
                            wait(dve, slots_mm, g2 + 1)
                            wait(dve, w_mm, g2 * NB)
                            scaled = chain.done(dve.tensor_scalar(sl[:, 0, :], E_, 1.0 / LO, -0.5 + 0.5 / LO, ALU.mult, ALU.add))
                            high = chain.done(dve.tensor_copy(whi[:, :], W_))
                            chain.wait(scaled)
                            rounded = chain.done(dve.tensor_scalar(sl[:, 1, :], sl[:, 0, :], ROUND, None, ALU.add))
                            chain.wait(high)
                            low = chain.done(dve.tensor_tensor(wlo[:, :], W_, whi[:, :], ALU.subtract))
                            chain.wait(rounded)
                            row = chain.done(dve.tensor_scalar(sl[:, 2, :], sl[:, 1, :], ROUND, None, ALU.subtract))
                            row16 = chain.done(dve.tensor_scalar(rowid[:, :], sl[:, 1, :], ROUND, None, ALU.subtract))
                            chain.wait(row)
                            column = chain.done(dve.scalar_tensor_tensor(out=sl[:, 3, :], in0=sl[:, 2, :], scalar=-float(LO), in1=E_,
                                                                         op0=ALU.mult, op1=ALU.add))
                            chain.wait(column)
                            chain.wait(chain.done(dve.tensor_scalar(colid[:, :], sl[:, 3, :], half_off[:, 0:1], None, ALU.add)))
                            for c in range(2 * LO):
                                ins = dve.tensor_scalar(Ylo[:, c, :], colid[:, :], float(c), None, ALU.is_equal)
                            onehot = chain.done(ins)
                            for c in range(P):
                                ins = dve.tensor_scalar(X[:, c, :], rowid[:, :], float(c), None, ALU.is_equal)
                            chain.wait(onehot)
                            dve.tensor_tensor(Yhi[:, :, :], Ylo[:, :, :], whi[:, :].unsqueeze(1).to_broadcast([P, 2 * LO, COLS]), ALU.mult)
                            dve.tensor_tensor(Ylo[:, :, :], Ylo[:, :, :], wlo[:, :].unsqueeze(1).to_broadcast([P, 2 * LO, COLS]),
                                              ALU.mult).then_inc(built, 1)
                        if active(s, 0):
                            for c in range(TILES):
                                touch(dve, sim_ev[c], g + 1, idle[:, 2 * c + q:2 * c + q + 1])
                                for j in range(HF):
                                    ins = dve.max(best[:, j // H, c * H + j % H, :], sim[:, c, j, :])
                            chain.wait(chain.done(ins))
                            for c in range(TILES):
                                for j in range(HF):
                                    ins = dve.max_index(bidx[:, j // H, c * H + j % H, :], best[:, j // H, c * H + j % H, :], sim[:, c, j, :])
                            ins.then_inc(axis_top, 1)
                            k = 0
                            for a0, a1, nb in AROWS:
                                n = (a1 - a0) * nb
                                ins = dve.tensor_tensor(cand[:, :, k:k + n].rearrange("p c (a b) -> p c a b", b=nb),
                                                        best[:, 0, :, a0:a1].unsqueeze(3).to_broadcast([P, CH, a1 - a0, nb]),
                                                        best[:, 1, :, 0:nb].unsqueeze(2).to_broadcast([P, CH, a1 - a0, nb]), ALU.add)
                                k += n
                            sums = chain.done(ins)
                            wait(dve, axis_top, g + 1)
                            wait(dve, e_done, g - 1)
                            dve.tensor_scalar(idx[:, q, 0, :, :], bidx[:, 0, :, :], float(NK), None, ALU.mult)
                            dve.tensor_copy(idx[:, q, 1, :, :], bidx[:, 1, :, :])
                            chain.wait(sums)
                            for m in range(CH):
                                ins = dve.max(top[:, m, :], cand[:, m, :])
                            chain.wait(chain.done(ins))
                            for m in range(CH):
                                dve.max_index(posu[:, q, m, :], top[:, m, :], cand[:, m, :])
                            wait(dve, exp_done, g - 1)
                            dve.tensor_tensor(gap[:, q, :, :], top[:, :, :], top[:, :, 0:1].to_broadcast([P, CH, TOP]),
                                              ALU.subtract).then_inc(gap_done, 1)
                        if active(s, 2):
                            wait(dve, up_mm, g2 + 1)
                            wait(dve, out_sent[q], out_count(s, q))
                            dve.scalar_tensor_tensor(out=ob[:, q, :], in0=up_p[:, :], scalar=1.0 / WSCALE,
                                                     in1=x_sb[:, bass.ds(g2 * SEQ, SEQ)], op0=ALU.mult, op1=ALU.add).then_inc(fin, 1)
                        chain.restart()

                    def out_count(s, q):
                        return (s - q) * 8 - 16

                    steps(dve, 3, body)


_INS = ['L0_attn_x', 'L0_attn_W_spec', 'L0_attn_W_decay', 'L0_attn_b_decay', 'L0_attn_freqs', 'L0_attn_W_out',
        'L0_ffn_w_q', 'L0_ffn_bn_gamma', 'L0_ffn_bn_beta', 'L0_ffn_keys', 'L0_ffn_down_embed', 'L0_ffn_up_embed']
_OUTS = [((GROUPS, SEQ, D), 'float32')]


def kernel(**inputs):
    import numpy as _np
    import concourse.bacc as _bacc
    from concourse import mybir as _mybir
    from concourse.bass_utils import run_bass_kernel_spmd as _run

    nc = _bacc.Bacc("TRN2", target_bir_lowering=False, num_devices=1)
    arrays, args = {}, []
    for name in _INS:
        v = _np.ascontiguousarray(inputs[name])
        arrays[f"in_{name}_dram"] = v
        args.append(nc.dram_tensor(f"in_{name}_dram", v.shape, _mybir.dt.from_np(v.dtype), kind="ExternalInput").ap())
    for i, (shape, dtype) in enumerate(_OUTS):
        dt = _mybir.dt.from_np(_np.dtype(dtype))
        args.append(nc.dram_tensor(f"out_{i}_dram", shape, dt, kind="ExternalOutput").ap())
    build(nc, *args)
    r = _run(nc, [arrays], core_ids=[0])
    got = tuple(r.results[0][f"out_{i}_dram"] for i in range(len(_OUTS)))
    return got[0]
```

```python
from contextlib import ExitStack
import math

import concourse.bass as bass
from concourse import mybir

ALU = mybir.AluOpType
ACT = mybir.ActivationFunctionType
AX = mybir.AxisListType
F32 = mybir.dt.float32
F16 = mybir.dt.float16
BF16 = mybir.dt.bfloat16
U32 = mybir.dt.uint32

P = 128
D = 128
SEQ = 512
GROUPS = 8
TILES = SEQ // P
NTOK = GROUPS * SEQ
F = 64
H = 8
KD = 128
NK = 32
TOP = 8
HF = 2 * H
BROWS = 64 + HF
LO = 8
CH = TILES * H
COLS = SEQ // 2
EPS = 1e-5
ROUND = 1.5 * 2.0 ** 23
COARSE = 1.5 * 2.0 ** 10
WSCALE = 2.0 ** 14
PAIRS = [(a, b) for a in range(TOP) for b in range(TOP) if (a + 1) * (b + 1) <= TOP]
NP = len(PAIRS)
SKIP = [(a + 1) * (b + 1) - 1 for a, b in PAIRS]
PLACE = [sum(TOP - k for k in SKIP[:c]) for c in range(NP + 1)]
AROWS = ((0, 1, 8), (1, 2, 4), (2, 4, 2), (4, 8, 1))


def wait(eng, sem, value):
    if isinstance(value, int) and value <= 0:
        return
    eng.wait_ge(sem, value)


class Chain:

    def __init__(self, eng, sem):
        self.eng, self.sem, self.n = eng, sem, 0

    def done(self, ins):
        ins.then_inc(self.sem, 1)
        self.n += 1
        return self.n

    def wait(self, n):
        self.eng.wait_ge(self.sem, n)

    def restart(self):
        if self.n:
            self.wait(self.n)
            self.eng.sem_clear(self.sem)
        self.n = 0


def touch(dve, sem, value, cell):
    wait(dve, sem, value)
    dve.memset(cell, 0.0)


def steps(eng, nstages, body):
    first = nstages - 1 + (nstages - 1) % 2
    last = GROUPS - GROUPS % 2
    for s in range(first):
        body(s, s % 2)
    with eng.Fori(first // 2, last // 2) as i:
        for q in range(2):
            body(i * 2 + q, q)
    for s in range(last, GROUPS + nstages - 1):
        body(s, s % 2)


def active(s, lag):
    return not isinstance(s, int) or 0 <= s - lag < GROUPS


def build(nc, x, w_spec, w_decay, b_decay, freqs, w_out, w_q, bn_gamma, bn_beta, keys, down, up, out):
    with ExitStack() as whole:
        def sb(name, shape, dt=F32, ctx=whole):
            return ctx.enter_context(nc.sbuf_tensor(name, shape, dt))

        def sem(name):
            return whole.enter_context(nc.semaphore(name))

        banks = [whole.enter_context(nc.psum_tensor(f"bank{i}", [P, 512], F32)) for i in range(8)]

        x_sb = sb("x_sb", [P, NTOK])
        xn2T_all = sb("xn2T_all", [P, NTOK])
        ident = sb("ident", [P, P])
        ones = sb("ones", [P, P])
        eps_row = sb("eps_row", [P, TILES])
        downT = sb("downT", [P, LO, P])
        up_sb = sb("up_sb", [P, LO, D])
        fold_M = sb("fold_M", [P, HF * NK])
        fold_b = sb("fold_b", [BROWS, HF * NK], BF16)
        ones_b = sb("ones_b", [BROWS, P], BF16)
        ident_w = sb("ident_w", [P, P])
        xs = sb("xs", [P, 2, SEQ])
        idle = sb("idle", [1, 2 * (TILES + 3)])
        half_pow = sb("half_pow", [P, 16])

        xs_in = [sem("xs_in0"), sem("xs_in1")]

        xr = x.rearrange("b (c p) d -> p (b c) d", p=P)

        with ExitStack() as ctx:
            def a(name, shape, dt=F32):
                return sb(name, shape, dt, ctx)

            wq_sb = a("wq_sb", [P, HF * KD])
            keys_sb = a("keys_sb", [P, 2, 2, KD])
            down_sb = a("down_sb", [P, LO, D])
            gb_sb = a("gb_sb", [2 * HF, KD])
            wspec = a("wspec", [P, 2 * F])
            wswap = a("wswap", [P, 2 * F])
            wdec = a("wdec", [P, 2 * F])
            wout = a("wout", [P, D])
            woutsw = a("woutsw", [P, D])
            bdec = a("bdec", [P, 1])
            freq = a("freq", [P, 1])
            rates = a("rates", [P, 5])
            sgn = a("sgn", [P, 1])
            pos_t = a("pos_t", [P, SEQ])
            ph = a("ph", [P, 5, SEQ])
            cosT = a("cosT", [P, SEQ])
            sinT = a("sinT", [P, SEQ])
            st1 = a("st1", [P, 2, TILES, 6])
            mv1 = a("mv1", [P, 2, TILES, 2])
            rs1 = a("rs1", [P, 2, TILES])
            xn1 = a("xn1", [P, 2, SEQ])
            xn1T = a("xn1T", [P, 2, SEQ])
            decay = a("decay", [P, 2, SEQ])
            rot1 = a("rot1", [P, 2, SEQ])
            rot2 = a("rot2", [P, 2, SEQ])
            pin = a("pin", [P, 2, SEQ])
            state = a("state", [P, 2, SEQ])
            gcos = a("gcos", [P, 2, SEQ])
            gsin = a("gsin", [P, 2, SEQ])
            st2 = a("st2", [P, 2, TILES, 6])
            mv2 = a("mv2", [P, 2, TILES, 2])
            ve1 = a("ve1", [P, 2, TILES])
            ve2 = a("ve2", [P, 2, TILES])
            rs2 = a("rs2", [P, 2, TILES])
            xn2 = a("xn2", [P, 2, TILES, D + 1])
            zeros = a("zeros", [P, D + 1])
            wqT = a("wqT", [P, HF, P])
            keysT = a("keysT", [P, HF, NK])
            gbT = a("gbT", [P, 2 * HF])
            gram = a("gram", [P, P + 1])
            prod = a("prod", [P, HF, P])
            stat = a("stat", [P, 7, HF])
            normA = a("normA", [P, HF])
            normB = a("normB", [P, BROWS])
            own_block = a("own_block", [BROWS, HF * NK])
            bias = a("bias", [BROWS, 2, HF * NK])
            keysA = a("keysA", [P, HF, NK])

            x_first, x_rest, f_in, w_in, w_late = sem("x_first"), sem("x_rest"), sem("f_in"), sem("w_in"), sem("w_late")
            consts, tables, table_step, sines = sem("consts"), sem("tables"), sem("table_step"), sem("sines")
            aggr1, rstd1, xn1_done = sem("aggr1"), sem("rstd1"), sem("xn1_done")
            xn1_psum, xn1T_done, spec_mm, decay_mm = sem("xn1_psum"), sem("xn1T_done"), sem("spec_mm"), sem("decay_mm")
            decay_done, rotated, pin_done, scanned = sem("decay_done"), sem("rotated"), sem("pin_done"), sem("scanned")
            rot_out, rot_out2, out_mm, x1_done = sem("rot_out"), sem("rot_out2"), sem("out_mm"), sem("x1_done")
            aggr2, rstd2, xn2_done = sem("aggr2"), sem("rstd2"), sem("xn2_done")
            xn2_psum, xn2T_done, gram_done = sem("xn2_psum"), sem("xn2T_done"), sem("gram_done")
            pool_chain, dve_chain = sem("pool_chain"), sem("dve_chain")
            late_mm, late_ev = sem("late_mm"), sem("late_ev")

            tp1, spec_u, spec_s, dec_p, out_p, tp2, gram_p = banks[:7]
            late_p = banks[7], tp1

            with nc.Block() as block:
                @block.sync
                def _(sp):
                    sp.dma_start(x_sb[:, 0:2 * SEQ].rearrange("p (t d) -> p t d", d=D), xr[:, 0:2 * TILES, :]).then_inc(x_first, 16)
                    for dst, src in ((wspec[:, :], w_spec), (wswap[:, 0:F], w_spec[:, F:2 * F]),
                                     (wswap[:, F:2 * F], w_spec[:, 0:F]), (wout[:, :], w_out),
                                     (woutsw[0:F, :], w_out[F:2 * F, :]), (woutsw[F:P, :], w_out[0:F, :])):
                        sp.dma_start(dst, src).then_inc(w_in, 16)
                    sp.dma_start(x_sb[:, 2 * SEQ:].rearrange("p (t d) -> p t d", d=D), xr[:, 2 * TILES:, :]).then_inc(x_rest, 16)
                    for dst, src in ((gb_sb[0:HF, :], bn_gamma.rearrange("(j k) -> j k", k=KD)),
                                     (gb_sb[HF:2 * HF, :], bn_beta.rearrange("(j k) -> j k", k=KD)),
                                     (keys_sb[:, :, :, :], keys.rearrange("(a h) k p d -> (h k) a p d", a=2)),
                                     (down_sb[:, :, :], down.rearrange("(c l) d -> c l d", l=LO)),
                                     (up_sb[:, :, :], up.rearrange("(c l) d -> c l d", l=LO)),
                                     (wq_sb[:, :], w_q)):
                        sp.dma_start(dst, src).then_inc(w_late, 16)

                TABLE_STEPS = 13
                LATE, LATE_FIRST = 9, 5
                W_FREQ, W_IN, W_LATE = 16 * 2, 16 * 10, 16 * 6

                @block.gpsimd
                def _(pool):
                    pool.memset(half_pow[:, :], -0.5)
                    pool.memset(eps_row[:, :], EPS)
                    pool.iota(pos_t[:, :], pattern=[[1, SEQ]], base=0, channel_multiplier=0,
                              allow_small_or_imprecise_dtypes=True).then_inc(tables, 1)
                    pool.memset(zeros[:, :], 0.0)
                    pool.memset(ones[:, :], 1.0)
                    pool.memset(xn2[:, :, :, D:D + 1], 1.0).then_inc(consts, 1)
                    pool.wait_ge(consts, 1)
                    pool.affine_select(out=ident[:, :], in_=zeros[:, 0:P], compare_op=ALU.not_equal, fill=1.0,
                                       base=0, pattern=[[-1, P]], channel_multiplier=1).then_inc(consts, 1)
                    pool.affine_select(out=ident_w[:, :], in_=zeros[:, 0:P], compare_op=ALU.not_equal, fill=WSCALE,
                                       base=0, pattern=[[-1, P]], channel_multiplier=1)

                    def body(s, q):
                        g, g1, g2, r = s, s - 1, s - 2, 1 - q
                        if active(s, 0):
                            wait(pool, aggr1, g + 1)
                            chain.wait(chain.done(pool.tensor_tensor(ve1[:, q, :], mv1[:, q, :, 1], eps_row[:, :], ALU.add)))
                            pool.tensor_tensor(rs1[:, q, :], ve1[:, q, :], half_pow[:, 0:TILES], ALU.pow).then_inc(rstd1, 1)
                        if active(s, 2):
                            wait(pool, aggr2, g2 + 1)
                            chain.wait(chain.done(pool.tensor_tensor(ve2[:, q, :], mv2[:, q, :, 1], eps_row[:, :], ALU.add)))
                            pool.tensor_tensor(rs2[:, q, :], ve2[:, q, :], half_pow[:, 0:TILES], ALU.pow).then_inc(rstd2, 1)
                        if active(s, 1):
                            wait(pool, rotated, g1 + 1)
                            wait(pool, scanned, g1 - 1)
                            pool.tensor_tensor(pin[:, r, :], rot1[:, r, :], rot2[:, r, :], ALU.add).then_inc(pin_done, 1)
                        if active(s, 1):
                            if isinstance(s, int) and s == 1:
                                pool.wait_ge(sines, 2)
                            wait(pool, scanned, g1 + 1)
                            wait(pool, out_mm, g1 - 1)
                            pool.tensor_tensor(gcos[:, r, :], state[:, r, :], cosT[:, :], ALU.mult).then_inc(rot_out, 1)
                        chain.restart()

                    chain = Chain(pool, pool_chain)
                    steps(pool, 3, body)

                @block.scalar
                def _(act):
                    for dst, src, to in ((freq[0:F, :], freqs.rearrange("(f a) -> f a", a=1), f_in),
                                         (freq[F:P, :], freqs.rearrange("(f a) -> f a", a=1), f_in),
                                         (wdec[:, 0:F], w_decay, w_in), (wdec[:, F:2 * F], w_decay, w_in),
                                         (bdec[0:F, :], b_decay.rearrange("(f a) -> f a", a=1), w_in),
                                         (bdec[F:P, :], b_decay.rearrange("(f a) -> f a", a=1), w_in)):
                        act.dma_start(dst, src).then_inc(to, 16)

                    def late_copies(n0, n1):
                        for n in range(n0, n1):
                            act.wait_ge(late_mm, n + 1)
                            bank = late_p[n % 2]
                            if n < 4:
                                dst, src = wqT[:, 4 * n:4 * n + 4, :], bank[:, :].rearrange("p (j d) -> p j d", d=P)
                            elif n < 6:
                                dst = keysT[:, (n - 4) * H:(n - 3) * H, :]
                                src = bank[:, 0:H * NK].rearrange("p (h k) -> p h k", k=NK)
                            elif n < 8:
                                dst, src = downT[:, 4 * (n - 6):4 * (n - 5), :], bank[:, :].rearrange("p (j d) -> p j d", d=P)
                            else:
                                dst, src = gbT[:, :], bank[:, 0:2 * HF]
                            act.copy(dst, src).then_inc(late_ev, 1)

                    def body(s, q):
                        g, g1, g2, r = s, s - 1, s - 2, 1 - q
                        if isinstance(s, int) and s == 1:
                            act.wait_ge(table_step, TABLE_STEPS)
                            act.activation(cosT[:, :], ph[:, 1, :], ACT.Sin, scale=6.2831850).then_inc(sines, 1)
                            act.activation(sinT[:, :], ph[:, 2, :], ACT.Sin, scale=sgn[:, 0:1]).then_inc(sines, 1)
                            act.wait_ge(w_in, W_IN)
                        if active(s, 1):
                            wait(act, decay_mm, g1 + 1)
                            wait(act, scanned, g1 - 1)
                            act.activation(decay[:, r, :], dec_p[:, :], ACT.Sigmoid, bias=bdec[:, 0:1]).then_inc(decay_done, 1)
                        if active(s, 0):
                            wait(act, xn1_psum, g + 1)
                            act.copy(xn1T[:, q, :], tp1[:, :]).then_inc(xn1T_done, 1)
                        if isinstance(s, int) and s == GROUPS:
                            late_copies(0, LATE_FIRST)
                        if isinstance(s, int) and s == GROUPS + 1:
                            late_copies(LATE_FIRST, LATE)
                        if active(s, 2):
                            wait(act, xn2_psum, g2 + 1)
                            act.copy(xn2T_all[:, bass.ds(g2 * SEQ, SEQ)], tp2[:, :]).then_inc(xn2T_done, 1)

                    steps(act, 3, body)

                @block.vector
                def _(dve):
                    done = [0]

                    def then(ins):
                        ins.then_inc(table_step, 1)
                        done[0] += 1
                        dve.wait_ge(table_step, done[0])

                    dve.memset(sgn[0:F, :], 6.2831850)
                    dve.memset(sgn[F:P, :], -6.2831850)

                    def rotation_tables():
                        dve.wait_ge(f_in, W_FREQ)
                        dve.wait_ge(tables, 1)
                        then(dve.tensor_scalar(rates[:, 0:1], freq[:, :], 0.1, None, ALU.mult))
                        then(dve.tensor_scalar(rates[:, 1:2], rates[:, 0:1], 1.0 / (2.0 * math.pi), None, ALU.mult))
                        then(dve.tensor_scalar(rates[:, 3:4], rates[:, 1:2], COARSE, COARSE, ALU.add, ALU.subtract))
                        then(dve.tensor_tensor(rates[:, 4:5], rates[:, 1:2], rates[:, 3:4], ALU.subtract))
                        then(dve.tensor_scalar(ph[:, 0, :], pos_t[:, :], rates[:, 3:4], None, ALU.mult))
                        then(dve.tensor_scalar(ph[:, 4, :], ph[:, 0, :], ROUND, ROUND, ALU.add, ALU.subtract))
                        then(dve.tensor_tensor(ph[:, 3, :], ph[:, 0, :], ph[:, 4, :], ALU.subtract))
                        then(dve.scalar_tensor_tensor(out=ph[:, 0, :], in0=pos_t[:, :], scalar=rates[:, 4:5], in1=ph[:, 3, :],
                                                      op0=ALU.mult, op1=ALU.add))
                        then(dve.tensor_scalar(ph[:, 4, :], ph[:, 0, :], ROUND, ROUND, ALU.add, ALU.subtract))
                        then(dve.tensor_tensor(ph[:, 2, :], ph[:, 0, :], ph[:, 4, :], ALU.subtract))
                        then(dve.tensor_scalar(ph[:, 3, :], ph[:, 0, :], 0.25, None, ALU.add))
                        then(dve.tensor_scalar(ph[:, 4, :], ph[:, 3, :], ROUND, ROUND, ALU.add, ALU.subtract))
                        then(dve.tensor_tensor(ph[:, 1, :], ph[:, 3, :], ph[:, 4, :], ALU.subtract))
                        assert done[0] == TABLE_STEPS

                    def body(s, q):
                        g, g1, g2, r = s, s - 1, s - 2, 1 - q

                        def tile(group, c):
                            return x_sb[:, bass.ds(group * SEQ + c * P, P)]

                        if active(s, 0):
                            if isinstance(s, int):
                                dve.wait_ge(x_first, 16)
                            else:
                                dve.wait_ge(x_rest, 16)
                            for c in range(TILES):
                                ins = dve.bn_stats(st1[:, q, c, :], tile(g, c))
                            chain.wait(chain.done(ins))
                            for c in range(TILES):
                                ins = dve.bn_aggr(mv1[:, q, c, :], st1[:, q, c, :])
                            ins.then_inc(aggr1, 1)
                        if active(s, 2):
                            wait(dve, out_mm, g2 + 1)
                            dve.tensor_tensor(x_sb[:, bass.ds(g2 * SEQ, SEQ)], out_p[:, :],
                                              x_sb[:, bass.ds(g2 * SEQ, SEQ)], ALU.add).then_inc(x1_done, 1)
                            touch(dve, x1_done, g2 + 1, idle[:, 2 * TILES + q:2 * TILES + q + 1])
                            for c in range(TILES):
                                ins = dve.bn_stats(st2[:, q, c, :], tile(g2, c))
                            chain.wait(chain.done(ins))
                            for c in range(TILES):
                                ins = dve.bn_aggr(mv2[:, q, c, :], st2[:, q, c, :])
                            ins.then_inc(aggr2, 1)
                        if isinstance(s, int) and s == 1:
                            dve.wait_ge(sines, 2)
                        if active(s, 1):
                            wait(dve, spec_mm, g1 + 1)
                            wait(dve, pin_done, g1 - 1)
                            dve.tensor_tensor(rot1[:, r, :], spec_u[:, :], cosT[:, :], ALU.mult)
                            dve.tensor_tensor(rot2[:, r, :], spec_s[:, :], sinT[:, :], ALU.mult).then_inc(rotated, 1)
                        if active(s, 2):
                            wait(dve, rstd2, g2 + 1)
                            for c in range(TILES):
                                ins = dve.tensor_scalar(xn2[:, q, c, 0:D], tile(g2, c), mv2[:, q, c, 0:1],
                                                        rs2[:, q, c:c + 1], ALU.subtract, ALU.mult)
                            ins.then_inc(xn2_done, 1)
                        if active(s, 0):
                            wait(dve, rstd1, g + 1)
                            wait(dve, xn1_psum, g - 1)
                            for c in range(TILES):
                                ins = dve.tensor_scalar(xn1[:, q, c * P:(c + 1) * P], tile(g, c), mv1[:, q, c, 0:1],
                                                        rs1[:, q, c:c + 1], ALU.subtract, ALU.mult)
                            ins.then_inc(xn1_done, 1)
                        if isinstance(s, int) and s == 0:
                            rotation_tables()
                        if active(s, 1):
                            wait(dve, pin_done, g1 + 1)
                            wait(dve, decay_done, g1 + 1)
                            wait(dve, rot_out, g1 - 1)
                            wait(dve, out_mm, g1 - 1)
                            dve.tensor_tensor_scan(out=state[:, r, :], data0=decay[:, r, :], data1=pin[:, r, :],
                                                   initial=0.0, op0=ALU.mult, op1=ALU.add).then_inc(scanned, 1)
                            wait(dve, scanned, g1 + 1)
                            dve.tensor_tensor(gsin[:, r, :], state[:, r, :], sinT[:, :], ALU.mult).then_inc(rot_out2, 1)
                        chain.restart()

                    chain = Chain(dve, dve_chain)
                    steps(dve, 3, body)

                @block.tensor
                def _(pe):
                    pe.wait_ge(consts, 2)
                    pe.matmul(gram_p[:, 0:P + 1], zeros[:, 0:P], zeros[:, :], start=True, stop=False)

                    def late_transposes(n0, n1):
                        for n in range(n0, n1):
                            if n >= 2:
                                pe.wait_ge(late_ev, n - 1)
                            bank = late_p[n % 2]
                            if n < 4:
                                for j in range(4):
                                    m = pe.transpose(bank[:, j * P:(j + 1) * P], wq_sb[:, (4 * n + j) * KD:(4 * n + j + 1) * KD], ident[:, :])
                            elif n < 6:
                                for b in range(2):
                                    m = pe.transpose(bank[:, b * P:(b + 1) * P], keys_sb[:, b, n - 4, :], ident[:, :])
                            elif n < 8:
                                for j in range(4):
                                    m = pe.transpose(bank[:, j * P:(j + 1) * P], down_sb[:, 4 * (n - 6) + j, :], ident[:, :])
                            else:
                                m = pe.transpose(bank[:, 0:2 * HF], gb_sb[:, :], ident[0:2 * HF, 0:2 * HF])
                            m.then_inc(late_mm, 1)

                    def body(s, q):
                        g, g1, g2, r = s, s - 1, s - 2, 1 - q
                        if isinstance(s, int) and s == GROUPS + 1:
                            late_transposes(LATE_FIRST, LATE)
                        if active(s, 2):
                            wait(pe, rot_out, g2 + 1)
                            wait(pe, rot_out2, g2 + 1)
                            wait(pe, x1_done, g2)
                            for c in range(TILES):
                                pe.matmul(out_p[:, c * D:(c + 1) * D], gcos[:, q, c * P:(c + 1) * P], wout[:, :], start=True, stop=False)
                                m = pe.matmul(out_p[:, c * D:(c + 1) * D], gsin[:, q, c * P:(c + 1) * P], woutsw[:, :], start=False, stop=True)
                            m.then_inc(out_mm, 1)
                        if active(s, 1):
                            if isinstance(s, int) and s == 1:
                                pe.wait_ge(w_in, W_IN)
                            wait(pe, xn1T_done, g1 + 1)
                            wait(pe, rotated, g1)
                            pe.matmul(spec_u[:, :], wspec[:, :], xn1T[:, r, :], start=True, stop=True)
                            pe.matmul(spec_s[:, :], wswap[:, :], xn1T[:, r, :], start=True, stop=True).then_inc(spec_mm, 1)
                            wait(pe, decay_done, g1)
                            pe.matmul(dec_p[:, :], wdec[:, :], xn1T[:, r, :], start=True, stop=True).then_inc(decay_mm, 1)
                        if active(s, 0):
                            wait(pe, xn1_done, g + 1)
                            wait(pe, xn1T_done, g)
                            for c in range(TILES):
                                m = pe.transpose(tp1[:, c * P:(c + 1) * P], xn1[:, q, c * P:(c + 1) * P], ident[:, :])
                            m.then_inc(xn1_psum, 1)
                        if isinstance(s, int) and s == GROUPS:
                            pe.wait_ge(w_late, W_LATE)
                            late_transposes(0, LATE_FIRST)
                        if active(s, 2):
                            wait(pe, xn2_done, g2 + 1)
                            for c in range(TILES):
                                pe.matmul(gram_p[:, 0:P + 1], xn2[:, q, c, 0:D], xn2[:, q, c, :], start=False, stop=False)
                            wait(pe, xn2T_done, g2)
                            for c in range(TILES):
                                m = pe.transpose(tp2[:, c * P:(c + 1) * P], xn2[:, q, c, 0:D], ident[:, :])
                            m.then_inc(xn2_psum, 1)

                    steps(pe, 3, body)
                    pe.matmul(gram_p[:, 0:P + 1], zeros[:, 0:P], zeros[:, :], start=False, stop=True).then_inc(gram_done, 1)

            fold_t, fold_rs, fold_m, fold_b1, fold_ev = (sem("fold_t"), sem("fold_rs"), sem("fold_m"), sem("fold_b1"),
                                                         sem("fold_ev"))
            fold = sem("fold")
            blocks = sem("blocks")
            PER = 3
            SETS = [(b, range(b * PER, min((b + 1) * PER, HF))) for b in range((HF + PER - 1) // PER)]
            with nc.Block() as block:
                @block.sync
                def _(sp):
                    sp.wait_ge(xn2T_done, GROUPS)
                    for q in range(2):
                        sp.dma_start(xs[:, q, :], xn2T_all[:, q * SEQ:(q + 1) * SEQ]).then_inc(xs_in[q], 16)

                @block.vector
                def _(dve):
                    done = [0]

                    def then(ins):
                        ins.then_inc(fold, 1)
                        done[0] += 1
                        dve.wait_ge(fold, done[0])

                    dve.wait_ge(gram_done, 1)
                    then(dve.tensor_scalar(gram[:, :], gram_p[:, 0:P + 1], 1.0 / NTOK, None, ALU.mult))
                    for b, js in SETS:
                        dve.wait_ge(fold_t, b + 1)
                        t = banks[b][:, 0:len(js) * (P + 1)].rearrange("p (j d) -> p j d", d=P + 1)
                        dve.tensor_tensor(prod[:, js[0]:js[-1] + 1, :], t[:, :, 0:P], wqT[:, js[0]:js[-1] + 1, :], ALU.mult)
                        ins = dve.tensor_copy(stat[:, 0, js[0]:js[-1] + 1], t[:, :, P])
                    then(ins)
                    then(dve.tensor_reduce(stat[:, 1, :], prod[:, :, :], AX.X, ALU.add))
                    then(dve.tensor_tensor(stat[:, 2, :], stat[:, 0, :], stat[:, 0, :], ALU.mult))
                    then(dve.tensor_tensor(stat[:, 3, :], stat[:, 1, :], stat[:, 2, :], ALU.subtract))
                    then(dve.tensor_scalar(stat[:, 4, :], stat[:, 3, :], 0.0, EPS, ALU.max, ALU.add))
                    dve.wait_ge(fold_rs, 1)
                    then(dve.tensor_tensor(normA[:, :], stat[:, 5, :], gbT[:, 0:HF], ALU.mult))
                    dve.tensor_tensor(keysA[:, :, :], keysT[:, :, :], normA[:, :].unsqueeze(2).to_broadcast([P, HF, NK]),
                                      ALU.mult).then_inc(fold, 1)
                    done[0] += 1
                    then(dve.tensor_tensor(stat[:, 6, :], stat[:, 0, :], normA[:, :], ALU.mult))
                    normB3 = normB[:, :].rearrange("p (n j) -> p n j", j=HF)[:, 0:BROWS // HF:2, :]
                    then(dve.tensor_tensor(normB3, gbT[:, HF:2 * HF].unsqueeze(1).to_broadcast([P, 3, HF]),
                                           stat[:, 6, :].unsqueeze(1).to_broadcast([P, 3, HF]), ALU.subtract))
                    assert done[0] == 10
                    dve.wait_ge(fold_b1, 1)
                    then(dve.tensor_tensor(bias[:, 0, :], banks[6][0:BROWS, :], own_block[:, :], ALU.mult))
                    then(dve.tensor_copy(fold_b[:, :], bias[:, 0, :]))
                    then(dve.tensor_tensor(bias[:, 1, :], bias[:, 0, :], fold_b[:, :], ALU.subtract))
                    then(dve.tensor_copy(fold_b[0:64, :], bias[0:64, 1, :]))
                    dve.tensor_tensor(fold_b[0:32, :], bias[0:32, 1, :], fold_b[0:32, :], ALU.subtract).then_inc(fold_ev, 1)

                @block.gpsimd
                def _(pool):
                    pool.memset(ones_b[:, :], 1.0)
                    pool.memset(normB[:, :], 0.0)
                    pool.memset(own_block[:, :], 0.0).then_inc(blocks, 1)
                    own = own_block[:, :].rearrange("p (j k) -> p j k", k=NK)
                    for n in range(3):
                        pool.wait_ge(blocks, n + 1)
                        pool.affine_select(out=own, in_=own, compare_op=ALU.not_equal, fill=1.0, base=-32 * n,
                                           pattern=[[-1, HF], [0, NK]], channel_multiplier=1).then_inc(blocks, 1)
                    pool.wait_ge(fold, 6)
                    pool.tensor_tensor(stat[:, 5, :], stat[:, 4, :], half_pow[:, :], ALU.pow).then_inc(fold_rs, 1)

                @block.tensor
                def _(pe):
                    pe.wait_ge(fold, 1)
                    for b, js in SETS:
                        for k, j in enumerate(js):
                            m = pe.matmul(banks[b][:, k * (P + 1):(k + 1) * (P + 1)], wq_sb[:, j * KD:(j + 1) * KD], gram[:, :],
                                          start=True, stop=True)
                        m.then_inc(fold_t, 1)
                    pe.wait_ge(fold, 8)
                    for j in range(HF):
                        m = pe.matmul(banks[5][:, j * NK:(j + 1) * NK], wqT[:, j, :], keysA[:, j, :], start=True, stop=True)
                    m.then_inc(fold_m, 1)
                    pe.wait_ge(fold, 10)
                    pe.matmul(banks[6][0:BROWS, :], normB[:, :], keysT[:, :, :].rearrange("p j k -> p (j k)"), start=True, stop=True).then_inc(fold_b1, 1)

                @block.scalar
                def _(act):
                    act.wait_ge(fold_m, 1)
                    act.copy(fold_M[:, :], banks[5][:, :]).then_inc(fold_ev, 1)

        with ExitStack() as ctx:
            def a(name, shape, dt=F32):
                return sb(name, shape, dt, ctx)

            RC, CC = 8, 2
            RS, CS = P // RC, 2 * LO // CC
            MID = (LO - 1) / 2.0

            sim = a("sim", [P, TILES, HF, NK])
            best = a("best", [P, 2, CH, TOP])
            bidx = a("bidx", [P, 2, CH, TOP], U32)
            idx = a("idx", [P, 2, 2, CH, TOP])
            cand = a("cand", [P, CH, NP])
            ecand = a("ecand", [P, CH, NP])
            top = a("top", [P, CH, TOP])
            posu = a("posu", [P, 2, CH, TOP], U32)
            gap = a("gap", [P, 2, CH, TOP])
            ex = a("ex", [P, CH, TOP])
            esum = a("esum", [P, CH])
            einv = a("einv", [P, CH])
            wslot = a("wslot", [P, CH, TOP])
            eslot = a("eslot", [P, CH, TOP])
            took = a("took", [P, PLACE[NP] * CH], F16)
            pair_off = a("pair_off", [P, NP])
            share = a("share", [P, 3, CH, TOP])
            sl = a("sl", [P, 3, COLS])
            rowid = a("rowid", [P, RC, COLS], F16)
            colid = a("colid", [P, CC, COLS], F16)
            whi = a("whi", [P, COLS], F16)
            wlo = a("wlo", [P, COLS], F16)
            half_off = a("half_off", [P, 1])
            unrow = a("unrow", [P, RC])
            low_off = a("low_off", [P, 1])
            round_up = a("round_up", [P, 1])
            one = a("one", [P, 1])
            X = a("X", [P, P, COLS], F16)
            Yhi = a("Yhi", [P, 2 * LO, COLS], F16)
            Ylo = a("Ylo", [P, 2 * LO, COLS], F16)
            act_g = a("act_g", [P, LO, SEQ])
            wsb = a("wsb", [P, LO, SEQ])

            simp, gp, wp, slot_p, up_p = banks[0:2], banks[2:4], banks[4:6], banks[6], banks[7]
            out_sent = sem("out_sent")
            sim_mm = [sem(f"sim_mm{c}") for c in range(TILES)]
            sim_ev = [sem(f"sim_ev{c}") for c in range(TILES)]
            g_mm, g_ev, w_mm, w_ev, wg_done, up_mm = sem("g_mm"), sem("g_ev"), sem("w_mm"), sem("w_ev"), sem("wg_done"), sem("up_mm")
            axis_top, gap_done, exp_done, w_done = sem("axis_top"), sem("gap_done"), sem("exp_done"), sem("w_done")
            e_done, slots_mm, slots_ev, idx_done = sem("e_done"), sem("slots_mm"), sem("slots_ev"), sem("idx_done")
            took_done, act_chain = sem("took_done"), sem("act_chain")
            built, fin = sem("built"), sem("fin")
            ACT_PAIRS = 8

            def taken(c):
                return took[:, PLACE[c] * CH:PLACE[c + 1] * CH].rearrange("p (m k) -> p m k", m=CH)

            NB = 8
            TB = COLS // NB
            half_ready = sem("half_ready")

            with nc.Block() as block:
                @block.sync
                def _(sp):
                    def body(s, q):
                        wait(sp, sim_mm[TILES - 1], s - 1)
                        sp.dma_start(xs[:, q, :], xn2T_all[:, bass.ds(s * SEQ, SEQ)]).then_inc(xs_in[q], 16)

                    with sp.Fori(1, GROUPS // 2) as i:
                        for q in range(2):
                            body(i * 2 + q, q)
                    sp.wait_ge(out_sent, 16 * GROUPS)

                @block.tensor
                def _(pe):
                    pe.wait_ge(fold_ev, 2)

                    def body(s, q):
                        g, g1, g2 = s, s - 1, s - 2
                        if active(s, 0):
                            pe.wait_ge(xs_in[q], xs_count(s, q))
                            for c in range(TILES):
                                wait(pe, sim_ev[(c + 2) % TILES], g + 1 if c >= 2 else g)
                                pe.matmul(simp[c % 2][:, :], xs[:, q, c * P:(c + 1) * P], fold_M[:, :], start=True, stop=False)
                                pe.matmul(simp[c % 2][:, :], ones_b[:, :], fold_b[:, :], start=False, stop=True).then_inc(sim_mm[c], 1)
                        if active(s, 2):
                            for l in range(LO):
                                wait(pe, g_ev, g2 * LO + max(l - 1, 0))
                                pe.matmul(gp[l % 2][:, :], downT[:, l, :], xn2T_all[:, bass.ds(g2 * SEQ, SEQ)],
                                          start=True, stop=True).then_inc(g_mm, 1)
                            wait(pe, built, g2 + 1)
                            for b in range(NB):
                                wait(pe, w_ev, g2 * NB + max(b - 1, 0))
                                for t in range(b * TB, (b + 1) * TB):
                                    o = wp[b % 2][:, (t % TB) * 2 * LO:(t % TB + 1) * 2 * LO]
                                    pe.matmul(o, X[:, :, t], Yhi[:, :, t], start=True, stop=False)
                                    m = pe.matmul(o, X[:, :, t], Ylo[:, :, t], start=False, stop=True)
                                m.then_inc(w_mm, 1)
                        if active(s, 1):
                            wait(pe, e_done, g1 + 1)
                            wait(pe, w_done, g1 + 1)
                            wait(pe, slots_ev, g1)
                            for m2 in range(2):
                                for k, src in enumerate((eslot, wslot)):
                                    m = pe.transpose(slot_p[:, (2 * k + m2) * P:(2 * k + m2 + 1) * P],
                                                     src[:, 2 * m2 * H:2 * (m2 + 1) * H, :].rearrange("p c k -> p (c k)"), ident[:, :])
                            m.then_inc(slots_mm, 1)
                        if active(s, 2):
                            wait(pe, fin, g2)
                            for c in range(TILES):
                                wait(pe, wg_done, g2 * TILES + c + 1)
                                pe.matmul(up_p[:, c * D:(c + 1) * D], ident_w[:, :], x_sb[:, bass.ds(g2 * SEQ + c * P, P)],
                                          start=True, stop=False)
                                for l in range(LO):
                                    m = pe.matmul(up_p[:, c * D:(c + 1) * D], wsb[:, l, c * P:(c + 1) * P], up_sb[:, l, :],
                                                  start=False, stop=(l == LO - 1))
                            m.then_inc(up_mm, 1)

                    def xs_count(s, q):
                        return (s - q) * 8 + 16

                    steps(pe, 3, body)

                @block.scalar
                def _(act):
                    chain = Chain(act, act_chain)

                    def body(s, q):
                        g, g1, g2 = s, s - 1, s - 2
                        if active(s, 0):
                            for c in range(TILES):
                                wait(act, sim_mm[c], g + 1)
                                wait(act, axis_top, g)
                                act.copy(sim[:, c, :, :], simp[c % 2][:, :].rearrange("p (j k) -> p j k", k=NK)).then_inc(sim_ev[c], 1)
                        if active(s, 2):
                            wait(act, wg_done, g2 * TILES)
                            for l in range(LO):
                                wait(act, g_mm, g2 * LO + l + 1)
                                act.activation(act_g[:, l, :], gp[l % 2][:, :], ACT.Gelu_apprx_tanh).then_inc(g_ev, 1)
                            wait(act, up_mm, g2)
                            for b in range(NB):
                                wait(act, w_mm, g2 * NB + b + 1)
                                t0 = (b * TB) % P
                                m2 = b * TB // P
                                dst = wsb[:, :, :].rearrange("p l (m r t) -> p m t r l", m=2, r=2)[:, m2, t0:t0 + TB, :, :]
                                act.copy(dst, wp[b % 2][:, :].rearrange("p (t r l) -> p t r l", r=2, l=LO)).then_inc(w_ev, 1)
                        if active(s, 1):
                            E_, W_ = slot_p[:, 0:COLS], slot_p[:, COLS:2 * COLS]
                            wait(act, slots_mm, g1 + 1)
                            wait(act, built, g1)
                            rounded = chain.done(act.activation(sl[:, 0, :], E_, ACT.Identity, bias=round_up[:, 0:1], scale=1.0 / LO))
                            act.activation(sl[:, 1, :], E_, ACT.Identity, bias=half_off[:, 0:1])
                            act.copy(whi[:, :], W_)
                            act.copy(sl[:, 2, :], W_)
                            chain.wait(rounded)
                            for j in range(RC):
                                ins = act.activation(rowid[:, j, :], sl[:, 0, :], ACT.Identity, bias=unrow[:, j:j + 1])
                            ins.then_inc(slots_ev, 1)
                        if active(s, 0):
                            wait(act, axis_top, g + 1)
                            wait(act, e_done, g - 1)
                            act.activation(idx[:, q, 0, :, :], bidx[:, 0, :, :], ACT.Copy, scale=float(NK))
                            act.activation(idx[:, q, 1, :, :], bidx[:, 1, :, :], ACT.Identity, bias=low_off[:, 0:1]).then_inc(idx_done, 1)
                            wait(act, gap_done, g + 1)
                            wait(act, e_done, g)
                            for c in range(ACT_PAIRS):
                                ins = act.activation(taken(c), posu[:, q, :, SKIP[c]:], ACT.Abs, bias=pair_off[:, c:c + 1])
                            chain.wait(chain.done(ins))
                            o = took[:, 0:PLACE[ACT_PAIRS] * CH]
                            act.activation(o, o, ACT.Relu, bias=one[:, 0:1], scale=-1.0).then_inc(took_done, 1)
                            wait(act, w_done, g)
                            act.activation(ex[:, :, :], gap[:, q, :, :], ACT.Exp).then_inc(exp_done, 1)
                        if active(s, 2):
                            wait(act, up_mm, g2 + 1)
                            act.activation(x_sb[:, bass.ds(g2 * SEQ, SEQ)], up_p[:, :], ACT.Copy, scale=1.0 / WSCALE).then_inc(fin, 1)
                            wait(act, fin, g2 + 1)
                            act.dma_start(out[bass.ds(g2, 1)].rearrange("b (c p) d -> p (b c) d", p=P),
                                          x_sb[:, bass.ds(g2 * SEQ, SEQ)].rearrange("p (c d) -> p c d", d=D)).then_inc(out_sent, 16)
                        chain.restart()

                    act.wait_ge(half_ready, 1)
                    steps(act, 3, body)

                @block.gpsimd
                def _(pool):
                    def body(s, q):
                        g1, g2, r = s - 1, s - 2, 1 - q
                        if active(s, 1):
                            wait(pool, gap_done, g1 + 1)
                            wait(pool, idx_done, g1 + 1)
                            k = 0
                            for a0, a1, nb in AROWS:
                                n = (a1 - a0) * nb
                                o = ecand[:, :, k:k + n].rearrange("p c (a b) -> p c a b", b=nb)
                                ia = idx[:, r, 0, :, a0:a1].unsqueeze(3).to_broadcast([P, CH, a1 - a0, nb])
                                ib = idx[:, r, 1, :, 0:nb].unsqueeze(2).to_broadcast([P, CH, a1 - a0, nb])
                                ins = pool.tensor_tensor(o, ia, ib, ALU.add)
                                k += n
                            for c in range(ACT_PAIRS, NP):
                                ins = pool.tensor_scalar(taken(c), posu[:, r, :, SKIP[c]:], float(c), None, ALU.is_equal)
                            chain.wait(chain.done(ins))
                            wait(pool, slots_mm, g1)

                            def add(c, shared, added):
                                chain.wait(max(shared, added))
                                return pool.tensor_tensor(eslot[:, :, SKIP[c]:], eslot[:, :, SKIP[c]:], share[:, c % 3, :, SKIP[c]:], ALU.add)

                            before = None
                            for c in range(NP):
                                if c == 0:
                                    wait(pool, took_done, g1 + 1)
                                dst = share[:, c % 3, :, SKIP[c]:] if c else eslot[:, :, :]
                                shared = chain.done(pool.tensor_tensor(dst, taken(c), ecand[:, :, c:c + 1].to_broadcast([P, CH, TOP - SKIP[c]]), ALU.mult))
                                if before is None:
                                    added = shared
                                else:
                                    added = chain.done(add(c - 1, before, added))
                                before = shared if c else None
                            add(NP - 1, before, added).then_inc(e_done, 1)
                            chain.restart()
                        if active(s, 2):
                            wait(pool, g_ev, (g2 + 1) * LO)
                            for c in range(TILES):
                                wait(pool, w_ev, g2 * NB + NB // 2 * (c // 2 + 1))
                                w = wsb[:, :, c * P:(c + 1) * P]
                                pool.tensor_tensor(w, w, act_g[:, :, c * P:(c + 1) * P], ALU.mult).then_inc(wg_done, 1)

                    chain = Chain(pool, pool_chain)
                    steps(pool, 3, body)

                @block.vector
                def _(dve):
                    dve.memset(low_off[:, :], -MID)
                    dve.memset(round_up[:, :], ROUND)
                    dve.memset(one[:, :], 1.0)
                    for c in range(NP):
                        dve.memset(pair_off[:, c:c + 1], -float(c))
                    for j in range(RC):
                        dve.memset(unrow[:, j:j + 1], -(ROUND + RS * j))
                    dve.memset(half_off[0:64, :], MID)
                    dve.memset(half_off[64:P, :], MID + LO).then_inc(half_ready, 1)
                    chain = Chain(dve, dve_chain)

                    def body(s, q):
                        g, g1, g2, r = s, s - 1, s - 2, 1 - q
                        if active(s, 2):
                            wait(dve, slots_ev, g2 + 1)
                            column = chain.done(dve.scalar_tensor_tensor(out=colid[:, 0, :], in0=rowid[:, 0, :], scalar=-float(LO),
                                                                         in1=sl[:, 1, :], op0=ALU.mult, op1=ALU.add))
                            wait(dve, w_mm, g2 * NB)
                            dve.tensor_tensor(wlo[:, :], sl[:, 2, :], whi[:, :], ALU.subtract)
                            chain.wait(column)
                            columns = chain.done(dve.tensor_scalar(colid[:, 1, :], colid[:, 0, :], float(CS), None, ALU.subtract))
                            Xc = X[:, :, :].rearrange("p (j i) t -> p i j t", j=RC)
                            for i in range(RS):
                                dve.tensor_scalar(Xc[:, i], rowid[:, :, :], float(i), None, ALU.is_equal)
                            chain.wait(columns)
                            Yc = Ylo[:, :, :].rearrange("p (j i) t -> p i j t", j=CC)
                            for i in range(CS):
                                ins = dve.tensor_scalar(Yc[:, i], colid[:, :, :], float(i), None, ALU.is_equal)
                            chain.wait(chain.done(ins))
                            dve.tensor_tensor(Yhi[:, :, :], Ylo[:, :, :], whi[:, :].unsqueeze(1).to_broadcast([P, 2 * LO, COLS]), ALU.mult)
                            dve.tensor_tensor(Ylo[:, :, :], Ylo[:, :, :], wlo[:, :].unsqueeze(1).to_broadcast([P, 2 * LO, COLS]),
                                              ALU.mult).then_inc(built, 1)
                        if active(s, 1):
                            wait(dve, exp_done, g1 + 1)
                            chain.wait(chain.done(dve.tensor_reduce(esum[:, :], ex[:, :, :], AX.X, ALU.add)))
                            chain.wait(chain.done(dve.reciprocal(einv[:, :], esum[:, :])))
                            wait(dve, slots_mm, g1)
                            dve.scalar_tensor_tensor(out=wslot[:, :, :], in0=ex[:, :, :], scalar=WSCALE,
                                                     in1=einv[:, :].unsqueeze(2).to_broadcast([P, CH, TOP]),
                                                     op0=ALU.mult, op1=ALU.mult).then_inc(w_done, 1)
                        if active(s, 0):
                            n = 2 * (TILES + 1)
                            touch(dve, idx_done, g, idle[:, n + q:n + q + 1])
                            touch(dve, e_done, g - 1, idle[:, n + 2 + q:n + 3 + q])
                            for c in range(TILES):
                                touch(dve, sim_ev[c], g + 1, idle[:, 2 * c + q:2 * c + q + 1])
                                for j in range(HF):
                                    ins = dve.max(best[:, j // H, c * H + j % H, :], sim[:, c, j, :])
                            chain.wait(chain.done(ins))
                            for c in range(TILES):
                                for j in range(HF):
                                    ins = dve.max_index(bidx[:, j // H, c * H + j % H, :], best[:, j // H, c * H + j % H, :], sim[:, c, j, :])
                            ins.then_inc(axis_top, 1)
                            k = 0
                            for a0, a1, nb in AROWS:
                                n = (a1 - a0) * nb
                                ins = dve.tensor_tensor(cand[:, :, k:k + n].rearrange("p c (a b) -> p c a b", b=nb),
                                                        best[:, 0, :, a0:a1].unsqueeze(3).to_broadcast([P, CH, a1 - a0, nb]),
                                                        best[:, 1, :, 0:nb].unsqueeze(2).to_broadcast([P, CH, a1 - a0, nb]), ALU.add)
                                k += n
                            sums = chain.done(ins)
                            chain.wait(sums)
                            for m in range(CH):
                                ins = dve.max(top[:, m, :], cand[:, m, :])
                            chain.wait(chain.done(ins))
                            for m in range(CH):
                                dve.max_index(posu[:, q, m, :], top[:, m, :], cand[:, m, :])
                            wait(dve, exp_done, g - 1)
                            dve.tensor_tensor(gap[:, q, :, :], top[:, :, :], top[:, :, 0:1].to_broadcast([P, CH, TOP]),
                                              ALU.subtract).then_inc(gap_done, 1)
                        chain.restart()

                    steps(dve, 3, body)


_INS = ['L0_attn_x', 'L0_attn_W_spec', 'L0_attn_W_decay', 'L0_attn_b_decay', 'L0_attn_freqs', 'L0_attn_W_out',
        'L0_ffn_w_q', 'L0_ffn_bn_gamma', 'L0_ffn_bn_beta', 'L0_ffn_keys', 'L0_ffn_down_embed', 'L0_ffn_up_embed']
_OUTS = [((GROUPS, SEQ, D), 'float32')]


def kernel(**inputs):
    import numpy as _np
    import concourse.bacc as _bacc
    from concourse import mybir as _mybir
    from concourse.bass_utils import run_bass_kernel_spmd as _run

    nc = _bacc.Bacc("TRN2", target_bir_lowering=False, num_devices=1)
    arrays, args = {}, []
    for name in _INS:
        v = _np.ascontiguousarray(inputs[name])
        arrays[f"in_{name}_dram"] = v
        args.append(nc.dram_tensor(f"in_{name}_dram", v.shape, _mybir.dt.from_np(v.dtype), kind="ExternalInput").ap())
    for i, (shape, dtype) in enumerate(_OUTS):
        dt = _mybir.dt.from_np(_np.dtype(dtype))
        args.append(nc.dram_tensor(f"out_{i}_dram", shape, dt, kind="ExternalOutput").ap())
    build(nc, *args)
    r = _run(nc, [arrays], core_ids=[0])
    got = tuple(r.results[0][f"out_{i}_dram"] for i in range(len(_OUTS)))
    return got[0]
```

```python
from contextlib import ExitStack
import math

import concourse.bass as bass
from concourse import mybir

ALU = mybir.AluOpType
ACT = mybir.ActivationFunctionType
AX = mybir.AxisListType
F32 = mybir.dt.float32
F16 = mybir.dt.float16
BF16 = mybir.dt.bfloat16
U32 = mybir.dt.uint32

P = 128
D = 128
SEQ = 512
GROUPS = 8
TILES = SEQ // P
NTOK = GROUPS * SEQ
F = 64
H = 8
KD = 128
NK = 32
TOP = 8
HF = 2 * H
BROWS = 64 + HF
LO = 8
CH = TILES * H
COLS = SEQ // 2
EPS = 1e-5
ROUND = 1.5 * 2.0 ** 23
COARSE = 1.5 * 2.0 ** 10
WSCALE = 2.0 ** 14
RC, CC = 8, 2
RS, CS = P // RC, 2 * LO // CC
MID = (LO - 1) / 2.0
PAIRS = [(a, b) for a in range(TOP) for b in range(TOP) if (a + 1) * (b + 1) <= TOP]
NP = len(PAIRS)
SKIP = [(a + 1) * (b + 1) - 1 for a, b in PAIRS]
PLACE = [sum(TOP - k for k in SKIP[:c]) for c in range(NP + 1)]
AROWS = ((0, 1, 8), (1, 2, 4), (2, 4, 2), (4, 8, 1))


def wait(eng, sem, value):
    if isinstance(value, int) and value <= 0:
        return
    eng.wait_ge(sem, value)


class Chain:

    def __init__(self, eng, sem):
        self.eng, self.sem, self.n = eng, sem, 0

    def done(self, ins):
        ins.then_inc(self.sem, 1)
        self.n += 1
        return self.n

    def wait(self, n):
        self.eng.wait_ge(self.sem, n)

    def restart(self):
        if self.n:
            self.wait(self.n)
            self.eng.sem_clear(self.sem)
        self.n = 0


def touch(dve, sem, value, cell):
    wait(dve, sem, value)
    dve.memset(cell, 0.0)


def steps(eng, nstages, body):
    first = nstages - 1 + (nstages - 1) % 2
    last = GROUPS - GROUPS % 2
    for s in range(first):
        body(s, s % 2)
    with eng.Fori(first // 2, last // 2) as i:
        for q in range(2):
            body(i * 2 + q, q)
    for s in range(last, GROUPS + nstages - 1):
        body(s, s % 2)


def active(s, lag):
    return not isinstance(s, int) or 0 <= s - lag < GROUPS


def tail(s):
    return isinstance(s, int) and s >= GROUPS


def portions(s):
    return ((0, 1), (1, 2)) if tail(s) else ((0, 2),)


def build(nc, x, w_spec, w_decay, b_decay, freqs, w_out, w_q, bn_gamma, bn_beta, keys, down, up, out):
    with ExitStack() as whole:
        def sb(name, shape, dt=F32, ctx=whole):
            return ctx.enter_context(nc.sbuf_tensor(name, shape, dt))

        def sem(name):
            return whole.enter_context(nc.semaphore(name))

        banks = [whole.enter_context(nc.psum_tensor(f"bank{i}", [P, 512], F32)) for i in range(8)]

        x_sb = sb("x_sb", [P, NTOK])
        xn2T_all = sb("xn2T_all", [P, NTOK])
        ident = sb("ident", [P, P])
        ones = sb("ones", [P, P])
        eps_row = sb("eps_row", [P, TILES])
        downT = sb("downT", [P, LO, P])
        up_sb = sb("up_sb", [P, LO, D])
        fold_M = sb("fold_M", [P, HF * NK])
        fold_b = sb("fold_b", [BROWS, HF * NK], BF16)
        ones_b = sb("ones_b", [BROWS, P], BF16)
        ident_w = sb("ident_w", [P, P])
        xs = sb("xs", [P, 2, SEQ])
        idle = sb("idle", [1, 2 * (TILES + 4)])
        half_pow = sb("half_pow", [P, 16])

        half_off = sb("half_off", [P, 1])
        unrow = sb("unrow", [P, RC])
        low_off = sb("low_off", [P, 1])
        round_up = sb("round_up", [P, 1])
        one = sb("one", [P, 1])
        pair_off = sb("pair_off", [P, NP])

        xs_in = [sem("xs_in0"), sem("xs_in1")]

        xr = x.rearrange("b (c p) d -> p (b c) d", p=P)

        with ExitStack() as ctx:
            def a(name, shape, dt=F32):
                return sb(name, shape, dt, ctx)

            wq_sb = a("wq_sb", [P, HF * KD])
            keys_sb = a("keys_sb", [P, 2, 2, KD])
            down_sb = a("down_sb", [P, LO, D])
            gb_sb = a("gb_sb", [2 * HF, KD])
            wspec = a("wspec", [P, 2 * F])
            wswap = a("wswap", [P, 2 * F])
            wdec = a("wdec", [P, 2 * F])
            wout = a("wout", [P, D])
            woutsw = a("woutsw", [P, D])
            bdec = a("bdec", [P, 1])
            freq = a("freq", [P, 1])
            rates = a("rates", [P, 5])
            sgn = a("sgn", [P, 1])
            pos_t = a("pos_t", [P, SEQ])
            ph = a("ph", [P, 5, SEQ])
            cosT = a("cosT", [P, SEQ])
            sinT = a("sinT", [P, SEQ])
            st1 = a("st1", [P, 2, TILES, 6])
            mv1 = a("mv1", [P, 2, TILES, 2])
            rs1 = a("rs1", [P, 2, TILES])
            xn1 = a("xn1", [P, 2, SEQ])
            xn1T = a("xn1T", [P, 2, SEQ])
            decay = a("decay", [P, 2, SEQ])
            rot1 = a("rot1", [P, 2, SEQ])
            rot2 = a("rot2", [P, 2, SEQ])
            pin = a("pin", [P, 2, SEQ])
            state = a("state", [P, 2, SEQ])
            gcos = a("gcos", [P, 2, SEQ])
            gsin = a("gsin", [P, 2, SEQ])
            st2 = a("st2", [P, 2, TILES, 6])
            mv2 = a("mv2", [P, 2, TILES, 2])
            ve1 = a("ve1", [P, 2, TILES])
            ve2 = a("ve2", [P, 2, TILES])
            rs2 = a("rs2", [P, 2, TILES])
            nm2 = a("nm2", [P, 2, TILES])
            sh2 = a("sh2", [P, 2, TILES])
            xn2 = a("xn2", [P, 2, TILES, D + 1])
            zeros = a("zeros", [P, D + 1])
            wqT = a("wqT", [P, HF, P])
            keysT = a("keysT", [P, HF, NK])
            gbT = a("gbT", [P, 2 * HF])
            gram = a("gram", [P, P + 1])
            prod = a("prod", [P, HF, P])
            stat = a("stat", [P, 7, HF])
            normA = a("normA", [P, HF])
            normB = a("normB", [P, BROWS])
            own_block = a("own_block", [BROWS, HF * NK])
            bias = a("bias", [BROWS, 2, HF * NK])
            keysA = a("keysA", [P, HF, NK])

            x_first, x_rest, f_in, w_in, w_late = sem("x_first"), sem("x_rest"), sem("f_in"), sem("w_in"), sem("w_late")
            consts, tables, table_step, sines = sem("consts"), sem("tables"), sem("table_step"), sem("sines")
            aggr1, rstd1, xn1_done = sem("aggr1"), sem("rstd1"), sem("xn1_done")
            xn1_psum, xn1T_done, spec_mm, decay_mm = sem("xn1_psum"), sem("xn1T_done"), sem("spec_mm"), sem("decay_mm")
            decay_done, rotated, pin_done, scanned = sem("decay_done"), sem("rotated"), sem("pin_done"), sem("scanned")
            rot_out, rot_out2, out_mm, x1_done = sem("rot_out"), sem("rot_out2"), sem("out_mm"), sem("x1_done")
            aggr2, rstd2, xn2_done = sem("aggr2"), sem("rstd2"), sem("xn2_done")
            xn2_psum, xn2T_done, gram_done = sem("xn2_psum"), sem("xn2T_done"), sem("gram_done")
            pool_chain, dve_chain = sem("pool_chain"), sem("dve_chain")
            late_mm, late_ev = sem("late_mm"), sem("late_ev")

            tp1, spec_u, spec_s, dec_p, out_p, tp2, gram_p = banks[:7]
            late_p = banks[7], tp1

            with nc.Block() as block:
                @block.sync
                def _(sp):
                    sp.dma_start(x_sb[:, 0:2 * SEQ].rearrange("p (t d) -> p t d", d=D), xr[:, 0:2 * TILES, :]).then_inc(x_first, 16)
                    for dst, src in ((wspec[:, :], w_spec), (wswap[:, 0:F], w_spec[:, F:2 * F]),
                                     (wswap[:, F:2 * F], w_spec[:, 0:F]), (wout[:, :], w_out),
                                     (woutsw[0:F, :], w_out[F:2 * F, :]), (woutsw[F:P, :], w_out[0:F, :])):
                        sp.dma_start(dst, src).then_inc(w_in, 16)
                    sp.dma_start(x_sb[:, 2 * SEQ:].rearrange("p (t d) -> p t d", d=D), xr[:, 2 * TILES:, :]).then_inc(x_rest, 16)
                    for dst, src in ((gb_sb[0:HF, :], bn_gamma.rearrange("(j k) -> j k", k=KD)),
                                     (gb_sb[HF:2 * HF, :], bn_beta.rearrange("(j k) -> j k", k=KD)),
                                     (keys_sb[:, :, :, :], keys.rearrange("(a h) k p d -> (h k) a p d", a=2)),
                                     (down_sb[:, :, :], down.rearrange("(c l) d -> c l d", l=LO)),
                                     (up_sb[:, :, :], up.rearrange("(c l) d -> c l d", l=LO)),
                                     (wq_sb[:, :], w_q)):
                        sp.dma_start(dst, src).then_inc(w_late, 16)

                TABLE_STEPS = 13
                LATE, LATE_FIRST = 9, 4
                W_FREQ, W_IN, W_LATE = 16 * 2, 16 * 10, 16 * 6

                @block.gpsimd
                def _(pool):
                    pool.memset(half_pow[:, :], -0.5)
                    pool.memset(eps_row[:, :], EPS)
                    pool.iota(pos_t[:, :], pattern=[[1, SEQ]], base=0, channel_multiplier=0,
                              allow_small_or_imprecise_dtypes=True).then_inc(tables, 1)
                    pool.memset(zeros[:, :], 0.0)
                    pool.memset(ones[:, :], 1.0)
                    pool.memset(xn2[:, :, :, D:D + 1], 1.0).then_inc(consts, 1)
                    pool.wait_ge(consts, 1)
                    pool.affine_select(out=ident[:, :], in_=zeros[:, 0:P], compare_op=ALU.not_equal, fill=1.0,
                                       base=0, pattern=[[-1, P]], channel_multiplier=1).then_inc(consts, 1)
                    pool.affine_select(out=ident_w[:, :], in_=zeros[:, 0:P], compare_op=ALU.not_equal, fill=WSCALE,
                                       base=0, pattern=[[-1, P]], channel_multiplier=1)

                    def body(s, q):
                        g, g1, g2, r = s, s - 1, s - 2, 1 - q
                        if active(s, 0):
                            wait(pool, aggr1, g + 1)
                            chain.wait(chain.done(pool.tensor_tensor(ve1[:, q, :], mv1[:, q, :, 1], eps_row[:, :], ALU.add)))
                            pool.tensor_tensor(rs1[:, q, :], ve1[:, q, :], half_pow[:, 0:TILES], ALU.pow).then_inc(rstd1, 1)
                        if active(s, 1):
                            wait(pool, rotated, g1 + 1)
                            wait(pool, scanned, g1 - 1)
                            pool.tensor_tensor(pin[:, r, :], rot1[:, r, :], rot2[:, r, :], ALU.add).then_inc(pin_done, 1)
                        if active(s, 1):
                            if isinstance(s, int) and s == 1:
                                pool.wait_ge(sines, 2)
                            wait(pool, scanned, g1 + 1)
                            wait(pool, out_mm, g1 - 1)
                            pool.tensor_tensor(gcos[:, r, :], state[:, r, :], cosT[:, :], ALU.mult).then_inc(rot_out, 1)
                        if active(s, 2):
                            wait(pool, aggr2, g2 + 1)
                            with_eps = chain.done(pool.tensor_tensor(ve2[:, q, :], mv2[:, q, :, 1], eps_row[:, :], ALU.add))
                            pool.tensor_scalar(nm2[:, q, :], mv2[:, q, :, 0], -1.0, None, ALU.mult)
                            chain.wait(with_eps)
                            chain.wait(chain.done(pool.tensor_tensor(rs2[:, q, :], ve2[:, q, :], half_pow[:, 0:TILES], ALU.pow)))
                            pool.tensor_tensor(sh2[:, q, :], nm2[:, q, :], rs2[:, q, :], ALU.mult).then_inc(rstd2, 1)
                        chain.restart()

                    chain = Chain(pool, pool_chain)
                    steps(pool, 3, body)

                @block.scalar
                def _(act):
                    for dst, src, to in ((freq[0:F, :], freqs.rearrange("(f a) -> f a", a=1), f_in),
                                         (freq[F:P, :], freqs.rearrange("(f a) -> f a", a=1), f_in),
                                         (wdec[:, 0:F], w_decay, w_in), (wdec[:, F:2 * F], w_decay, w_in),
                                         (bdec[0:F, :], b_decay.rearrange("(f a) -> f a", a=1), w_in),
                                         (bdec[F:P, :], b_decay.rearrange("(f a) -> f a", a=1), w_in)):
                        act.dma_start(dst, src).then_inc(to, 16)

                    def late_copies(n0, n1):
                        for n in range(n0, n1):
                            act.wait_ge(late_mm, n + 1)
                            bank = late_p[n % 2]
                            if n < 4:
                                dst, src = wqT[:, 4 * n:4 * n + 4, :], bank[:, :].rearrange("p (j d) -> p j d", d=P)
                            elif n < 6:
                                dst = keysT[:, (n - 4) * H:(n - 3) * H, :]
                                src = bank[:, 0:H * NK].rearrange("p (h k) -> p h k", k=NK)
                            elif n < 8:
                                dst, src = downT[:, 4 * (n - 6):4 * (n - 5), :], bank[:, :].rearrange("p (j d) -> p j d", d=P)
                            else:
                                dst, src = gbT[:, :], bank[:, 0:2 * HF]
                            act.copy(dst, src).then_inc(late_ev, 1)

                    def body(s, q):
                        g, g1, g2, g3, r = s, s - 1, s - 2, s - 3, 1 - q
                        if isinstance(s, int) and s == 1:
                            act.wait_ge(table_step, TABLE_STEPS)
                            act.activation(cosT[:, :], ph[:, 1, :], ACT.Sin, scale=6.2831850).then_inc(sines, 1)
                            act.activation(sinT[:, :], ph[:, 2, :], ACT.Sin, scale=sgn[:, 0:1]).then_inc(sines, 1)
                            act.wait_ge(w_in, W_IN)
                        if active(s, 1):
                            wait(act, decay_mm, g1 + 1)
                            wait(act, scanned, g1 - 1)
                            act.activation(decay[:, r, :], dec_p[:, :], ACT.Sigmoid, bias=bdec[:, 0:1]).then_inc(decay_done, 1)
                        if active(s, 3):
                            wait(act, xn2_psum, g3 + 1)
                            act.copy(xn2T_all[:, bass.ds(g3 * SEQ, SEQ)], tp2[:, :]).then_inc(xn2T_done, 1)
                        if active(s, 0):
                            wait(act, xn1_psum, g + 1)
                            act.copy(xn1T[:, q, :], tp1[:, :]).then_inc(xn1T_done, 1)
                        if isinstance(s, int) and s == GROUPS:
                            late_copies(0, LATE_FIRST)
                        if isinstance(s, int) and s == GROUPS + 1:
                            late_copies(LATE_FIRST, LATE)
                        if active(s, 2) and not (isinstance(s, int) and s >= GROUPS):
                            wait(act, rstd2, g2 + 1)
                            for c in range(TILES):
                                ins = act.activation(xn2[:, q, c, 0:D], x_sb[:, bass.ds(g2 * SEQ + c * P, P)], ACT.Identity,
                                                     scale=rs2[:, q, c:c + 1], bias=sh2[:, q, c:c + 1])
                            ins.then_inc(xn2_done, 1)

                    steps(act, 4, body)

                @block.vector
                def _(dve):
                    done = [0]

                    def then(ins):
                        ins.then_inc(table_step, 1)
                        done[0] += 1
                        dve.wait_ge(table_step, done[0])

                    dve.memset(half_off[0:64, :], MID)
                    dve.memset(half_off[64:P, :], MID + LO)
                    dve.memset(sgn[0:F, :], 6.2831850)
                    dve.memset(sgn[F:P, :], -6.2831850)

                    def rotation_tables():
                        dve.wait_ge(f_in, W_FREQ)
                        dve.wait_ge(tables, 1)
                        then(dve.tensor_scalar(rates[:, 0:1], freq[:, :], 0.1, None, ALU.mult))
                        then(dve.tensor_scalar(rates[:, 1:2], rates[:, 0:1], 1.0 / (2.0 * math.pi), None, ALU.mult))
                        then(dve.tensor_scalar(rates[:, 3:4], rates[:, 1:2], COARSE, COARSE, ALU.add, ALU.subtract))
                        then(dve.tensor_tensor(rates[:, 4:5], rates[:, 1:2], rates[:, 3:4], ALU.subtract))
                        then(dve.tensor_scalar(ph[:, 0, :], pos_t[:, :], rates[:, 3:4], None, ALU.mult))
                        then(dve.tensor_scalar(ph[:, 4, :], ph[:, 0, :], ROUND, ROUND, ALU.add, ALU.subtract))
                        then(dve.tensor_tensor(ph[:, 3, :], ph[:, 0, :], ph[:, 4, :], ALU.subtract))
                        then(dve.scalar_tensor_tensor(out=ph[:, 0, :], in0=pos_t[:, :], scalar=rates[:, 4:5], in1=ph[:, 3, :],
                                                      op0=ALU.mult, op1=ALU.add))
                        then(dve.tensor_scalar(ph[:, 4, :], ph[:, 0, :], ROUND, ROUND, ALU.add, ALU.subtract))
                        then(dve.tensor_tensor(ph[:, 2, :], ph[:, 0, :], ph[:, 4, :], ALU.subtract))
                        then(dve.tensor_scalar(ph[:, 3, :], ph[:, 0, :], 0.25, None, ALU.add))
                        then(dve.tensor_scalar(ph[:, 4, :], ph[:, 3, :], ROUND, ROUND, ALU.add, ALU.subtract))
                        then(dve.tensor_tensor(ph[:, 1, :], ph[:, 3, :], ph[:, 4, :], ALU.subtract))
                        assert done[0] == TABLE_STEPS

                    def times_sines(g1, r):
                        wait(dve, out_mm, g1 - 1)
                        wait(dve, scanned, g1 + 1)
                        dve.tensor_tensor(gsin[:, r, :], state[:, r, :], sinT[:, :], ALU.mult).then_inc(rot_out2, 1)

                    def body(s, q):
                        g, g1, g2, r = s, s - 1, s - 2, 1 - q

                        def tile(group, c):
                            return x_sb[:, bass.ds(group * SEQ + c * P, P)]

                        if active(s, 0):
                            if isinstance(s, int):
                                dve.wait_ge(x_first, 16)
                            else:
                                dve.wait_ge(x_rest, 16)
                            for c in range(TILES):
                                ins = dve.bn_stats(st1[:, q, c, :], tile(g, c))
                            chain.wait(chain.done(ins))
                            for c in range(TILES):
                                ins = dve.bn_aggr(mv1[:, q, c, :], st1[:, q, c, :])
                            ins.then_inc(aggr1, 1)
                        if isinstance(s, int) and s == 1:
                            dve.wait_ge(sines, 2)
                        if active(s, 1):
                            wait(dve, spec_mm, g1 + 1)
                            wait(dve, pin_done, g1 - 1)
                            dve.tensor_tensor(rot1[:, r, :], spec_u[:, :], cosT[:, :], ALU.mult)
                            dve.tensor_tensor(rot2[:, r, :], spec_s[:, :], sinT[:, :], ALU.mult).then_inc(rotated, 1)
                        if active(s, 0):
                            wait(dve, rstd1, g + 1)
                            wait(dve, xn1_psum, g - 1)
                            for c in range(TILES):
                                ins = dve.tensor_scalar(xn1[:, q, c * P:(c + 1) * P], tile(g, c), mv1[:, q, c, 0:1],
                                                        rs1[:, q, c:c + 1], ALU.subtract, ALU.mult)
                            ins.then_inc(xn1_done, 1)
                        if isinstance(s, int) and s == 0:
                            rotation_tables()
                        if active(s, 1):
                            wait(dve, pin_done, g1 + 1)
                            wait(dve, decay_done, g1 + 1)
                            wait(dve, rot_out, g1 - 1)
                            dve.tensor_tensor_scan(out=state[:, r, :], data0=decay[:, r, :], data1=pin[:, r, :],
                                                   initial=0.0, op0=ALU.mult, op1=ALU.add).then_inc(scanned, 1)
                        last = isinstance(s, int) and s >= GROUPS
                        if active(s, 1) and last:
                            times_sines(g1, r)
                        if active(s, 2):
                            wait(dve, out_mm, g2 + 1)
                            dve.tensor_tensor(x_sb[:, bass.ds(g2 * SEQ, SEQ)], out_p[:, :],
                                              x_sb[:, bass.ds(g2 * SEQ, SEQ)], ALU.add).then_inc(x1_done, 1)
                            touch(dve, x1_done, g2 + 1, idle[:, 2 * TILES + q:2 * TILES + q + 1])
                            for c in range(TILES):
                                ins = dve.bn_stats(st2[:, q, c, :], tile(g2, c))
                            chain.wait(chain.done(ins))
                            for c in range(TILES):
                                ins = dve.bn_aggr(mv2[:, q, c, :], st2[:, q, c, :])
                            ins.then_inc(aggr2, 1)
                        if active(s, 1) and not last:
                            times_sines(g1, r)
                        if active(s, 2) and last:
                            wait(dve, rstd2, g2 + 1)
                            for c in range(TILES):
                                ins = dve.tensor_scalar(xn2[:, q, c, 0:D], tile(g2, c), rs2[:, q, c:c + 1],
                                                        sh2[:, q, c:c + 1], ALU.mult, ALU.add)
                            ins.then_inc(xn2_done, 1)
                        chain.restart()

                    chain = Chain(dve, dve_chain)
                    steps(dve, 3, body)

                @block.tensor
                def _(pe):
                    pe.wait_ge(consts, 2)
                    pe.matmul(gram_p[:, 0:P + 1], zeros[:, 0:P], zeros[:, :], start=True, stop=False)

                    def late_transposes(n0, n1):
                        pe.wait_ge(w_late, W_LATE)
                        for n in range(n0, n1):
                            if n >= 2:
                                pe.wait_ge(late_ev, n - 1)
                            bank = late_p[n % 2]
                            if n < 4:
                                for j in range(4):
                                    m = pe.transpose(bank[:, j * P:(j + 1) * P], wq_sb[:, (4 * n + j) * KD:(4 * n + j + 1) * KD], ident[:, :])
                            elif n < 6:
                                for b in range(2):
                                    m = pe.transpose(bank[:, b * P:(b + 1) * P], keys_sb[:, b, n - 4, :], ident[:, :])
                            elif n < 8:
                                for j in range(4):
                                    m = pe.transpose(bank[:, j * P:(j + 1) * P], down_sb[:, 4 * (n - 6) + j, :], ident[:, :])
                            else:
                                m = pe.transpose(bank[:, 0:2 * HF], gb_sb[:, :], ident[0:2 * HF, 0:2 * HF])
                            m.then_inc(late_mm, 1)

                    def norm2_products(g3, r):
                        wait(pe, xn2_done, g3 + 1)
                        for c in range(TILES):
                            pe.matmul(gram_p[:, 0:P + 1], xn2[:, r, c, 0:D], xn2[:, r, c, :], start=False, stop=False)
                        wait(pe, xn2T_done, g3)
                        for c in range(TILES):
                            m = pe.transpose(tp2[:, c * P:(c + 1) * P], xn2[:, r, c, 0:D], ident[:, :])
                        m.then_inc(xn2_psum, 1)

                    def state_product(g2, q):
                        wait(pe, rot_out, g2 + 1)
                        wait(pe, rot_out2, g2 + 1)
                        wait(pe, x1_done, g2)
                        for c in range(TILES):
                            pe.matmul(out_p[:, c * D:(c + 1) * D], gcos[:, q, c * P:(c + 1) * P], wout[:, :], start=True, stop=False)
                            m = pe.matmul(out_p[:, c * D:(c + 1) * D], gsin[:, q, c * P:(c + 1) * P], woutsw[:, :], start=False, stop=True)
                        m.then_inc(out_mm, 1)

                    def body(s, q):
                        g, g1, g2, g3, r = s, s - 1, s - 2, s - 3, 1 - q
                        if active(s, 1):
                            if isinstance(s, int) and s == 1:
                                pe.wait_ge(w_in, W_IN)
                            wait(pe, xn1T_done, g1 + 1)
                            wait(pe, rotated, g1)
                            pe.matmul(spec_u[:, :], wspec[:, :], xn1T[:, r, :], start=True, stop=True)
                            pe.matmul(spec_s[:, :], wswap[:, :], xn1T[:, r, :], start=True, stop=True).then_inc(spec_mm, 1)
                            wait(pe, decay_done, g1)
                            pe.matmul(dec_p[:, :], wdec[:, :], xn1T[:, r, :], start=True, stop=True).then_inc(decay_mm, 1)
                        if active(s, 2):
                            state_product(g2, q)
                        if active(s, 3):
                            norm2_products(g3, r)
                        if active(s, 0):
                            wait(pe, xn1_done, g + 1)
                            wait(pe, xn1T_done, g)
                            for c in range(TILES):
                                m = pe.transpose(tp1[:, c * P:(c + 1) * P], xn1[:, q, c * P:(c + 1) * P], ident[:, :])
                            m.then_inc(xn1_psum, 1)
                        if isinstance(s, int) and s == GROUPS:
                            late_transposes(0, LATE_FIRST)
                        if isinstance(s, int) and s == GROUPS + 1:
                            late_transposes(LATE_FIRST, LATE)

                    steps(pe, 4, body)
                    pe.matmul(gram_p[:, 0:P + 1], zeros[:, 0:P], zeros[:, :], start=False, stop=True).then_inc(gram_done, 1)

            fold_t, fold_rs, fold_m, fold_b1, fold_ev = (sem("fold_t"), sem("fold_rs"), sem("fold_m"), sem("fold_b1"),
                                                         sem("fold_ev"))
            fold = sem("fold")
            blocks = sem("blocks")
            KEEP_BUSY = 8
            PER = 3
            SETS = [(b, range(b * PER, min((b + 1) * PER, HF))) for b in range((HF + PER - 1) // PER)]
            with nc.Block() as block:
                @block.sync
                def _(sp):
                    sp.wait_ge(xn2T_done, GROUPS)
                    for q in range(2):
                        sp.dma_start(xs[:, q, :], xn2T_all[:, q * SEQ:(q + 1) * SEQ]).then_inc(xs_in[q], 16)

                @block.vector
                def _(dve):
                    done = [0]

                    def then(ins):
                        ins.then_inc(fold, 1)
                        done[0] += 1
                        dve.wait_ge(fold, done[0])

                    dve.wait_ge(gram_done, 1)
                    then(dve.tensor_scalar(gram[:, :], gram_p[:, 0:P + 1], 1.0 / NTOK, None, ALU.mult))
                    for b, js in SETS:
                        dve.wait_ge(fold_t, b + 1)
                        t = banks[b][:, 0:len(js) * (P + 1)].rearrange("p (j d) -> p j d", d=P + 1)
                        dve.tensor_tensor(prod[:, js[0]:js[-1] + 1, :], t[:, :, 0:P], wqT[:, js[0]:js[-1] + 1, :], ALU.mult)
                        ins = dve.tensor_copy(stat[:, 0, js[0]:js[-1] + 1], t[:, :, P])
                    then(ins)
                    then(dve.tensor_reduce(stat[:, 1, :], prod[:, :, :], AX.X, ALU.add))
                    then(dve.tensor_tensor(stat[:, 2, :], stat[:, 0, :], stat[:, 0, :], ALU.mult))
                    then(dve.tensor_tensor(stat[:, 3, :], stat[:, 1, :], stat[:, 2, :], ALU.subtract))
                    then(dve.tensor_scalar(stat[:, 4, :], stat[:, 3, :], 0.0, EPS, ALU.max, ALU.add))
                    dve.wait_ge(fold_rs, 1)
                    then(dve.tensor_tensor(normA[:, :], stat[:, 5, :], gbT[:, 0:HF], ALU.mult))
                    then(dve.tensor_tensor(stat[:, 6, :], stat[:, 0, :], normA[:, :], ALU.mult))
                    normB3 = normB[:, :].rearrange("p (n j) -> p n j", j=HF)[:, 0:BROWS // HF:2, :]
                    then(dve.tensor_tensor(normB3, gbT[:, HF:2 * HF].unsqueeze(1).to_broadcast([P, 3, HF]),
                                           stat[:, 6, :].unsqueeze(1).to_broadcast([P, 3, HF]), ALU.subtract))
                    then(dve.tensor_tensor(keysA[:, :, :], keysT[:, :, :], normA[:, :].unsqueeze(2).to_broadcast([P, HF, NK]), ALU.mult))
                    assert done[0] == 10
                    dve.wait_ge(fold_b1, 1)
                    then(dve.tensor_tensor(bias[:, 0, :], banks[6][0:BROWS, :], own_block[:, :], ALU.mult))
                    then(dve.tensor_copy(fold_b[:, :], bias[:, 0, :]))
                    then(dve.tensor_tensor(bias[:, 1, :], bias[:, 0, :], fold_b[:, :], ALU.subtract))
                    then(dve.tensor_copy(fold_b[0:64, :], bias[0:64, 1, :]))
                    dve.tensor_tensor(fold_b[0:32, :], bias[0:32, 1, :], fold_b[0:32, :], ALU.subtract).then_inc(fold_ev, 1)

                @block.gpsimd
                def _(pool):
                    pool.memset(ones_b[:, :], 1.0)
                    pool.memset(normB[:, :], 0.0)
                    pool.memset(own_block[:, :], 0.0).then_inc(blocks, 1)
                    own = own_block[:, :].rearrange("p (j k) -> p j k", k=NK)
                    for n in range(3):
                        pool.wait_ge(blocks, n + 1)
                        pool.affine_select(out=own, in_=own, compare_op=ALU.not_equal, fill=1.0, base=-32 * n,
                                           pattern=[[-1, HF], [0, NK]], channel_multiplier=1).then_inc(blocks, 1)
                    pool.memset(low_off[:, :], -MID)
                    pool.memset(round_up[:, :], ROUND)
                    pool.memset(one[:, :], 1.0)
                    for c in range(NP):
                        pool.memset(pair_off[:, c:c + 1], -float(c))
                    for j in range(RC):
                        pool.memset(unrow[:, j:j + 1], -(ROUND + RS * j))
                    pool.wait_ge(fold, 6)
                    pool.tensor_tensor(stat[:, 5, :], stat[:, 4, :], half_pow[:, :], ALU.pow).then_inc(fold_rs, 1)

                @block.tensor
                def _(pe):
                    pe.wait_ge(fold, 1)
                    for b, js in SETS:
                        for k, j in enumerate(js):
                            m = pe.matmul(banks[b][:, k * (P + 1):(k + 1) * (P + 1)], wq_sb[:, j * KD:(j + 1) * KD], gram[:, :],
                                          start=True, stop=True)
                        m.then_inc(fold_t, 1)
                    for n in range(KEEP_BUSY):
                        pe.matmul(banks[7][:, :], ident[:, :], keysT[:, :, :].rearrange("p j k -> p (j k)"), start=True, stop=True)
                    pe.wait_ge(fold, 9)
                    pe.matmul(banks[6][0:BROWS, :], normB[:, :], keysT[:, :, :].rearrange("p j k -> p (j k)"), start=True, stop=True).then_inc(fold_b1, 1)
                    pe.wait_ge(fold, 10)
                    for j in range(HF):
                        m = pe.matmul(banks[5][:, j * NK:(j + 1) * NK], wqT[:, j, :], keysA[:, j, :], start=True, stop=True)
                    m.then_inc(fold_m, 1)

                @block.scalar
                def _(act):
                    act.wait_ge(fold_m, 1)
                    act.copy(fold_M[:, :], banks[5][:, :]).then_inc(fold_ev, 1)

        with ExitStack() as ctx:
            def a(name, shape, dt=F32):
                return sb(name, shape, dt, ctx)

            sim = a("sim", [P, TILES, HF, NK])
            best = a("best", [P, 2, CH, TOP])
            bidx = a("bidx", [P, 2, CH, TOP], U32)
            idx = a("idx", [P, 2, 2, CH, TOP])
            cand = a("cand", [P, CH, NP])
            ecand = a("ecand", [P, CH, NP])
            top = a("top", [P, CH, TOP])
            posu = a("posu", [P, 2, CH, TOP], U32)
            gap = a("gap", [P, 2, CH, TOP])
            ex = a("ex", [P, CH, TOP])
            esum = a("esum", [P, CH])
            einv = a("einv", [P, CH])
            wslot = a("wslot", [P, CH, TOP])
            eslot = a("eslot", [P, CH, TOP])
            took = a("took", [P, PLACE[NP] * CH], F16)
            share = a("share", [P, 3, CH, TOP])
            sl = a("sl", [P, 3, COLS])
            rowid = a("rowid", [P, RC, COLS], F16)
            colid = a("colid", [P, CC, COLS], F16)
            whi = a("whi", [P, COLS], F16)
            wlo = a("wlo", [P, COLS], F16)
            X = a("X", [P, P, COLS], F16)
            Yhi = a("Yhi", [P, 2 * LO, COLS], F16)
            Ylo = a("Ylo", [P, 2 * LO, COLS], F16)
            act_g = a("act_g", [P, LO, SEQ])
            wsb = a("wsb", [P, LO, SEQ])

            simp, gp, wp, slot_p, up_p = banks[0:2], banks[2:4], banks[4:6], banks[6], banks[7]
            out_sent = sem("out_sent")
            sim_mm = [sem(f"sim_mm{c}") for c in range(TILES)]
            sim_ev = [sem(f"sim_ev{c}") for c in range(TILES)]
            g_mm, g_ev, w_mm, w_ev, up_mm = sem("g_mm"), sem("g_ev"), sem("w_mm"), sem("w_ev"), sem("up_mm")
            wg_done, wg_dve = sem("wg_done"), sem("wg_dve")
            axis_top, gap_done, exp_done, w_done = sem("axis_top"), sem("gap_done"), sem("exp_done"), sem("w_done")
            ranked, low_done, inverted = sem("ranked"), sem("low_done"), sem("inverted")
            e_done, slots_mm, slots_ev, idx_done = sem("e_done"), sem("slots_mm"), sem("slots_ev"), sem("idx_done")
            took_done, act_chain, first_numbers = sem("took_done"), sem("act_chain"), sem("first_numbers")
            built, fin = sem("built"), sem("fin")
            ACT_PAIRS = 8

            def taken(c):
                return took[:, PLACE[c] * CH:PLACE[c + 1] * CH].rearrange("p (m k) -> p m k", m=CH)

            def pair_numbers(eng, r, h):
                nh = h.stop - h.start
                k = 0
                for a0, a1, nb in AROWS:
                    n = (a1 - a0) * nb
                    o = ecand[:, h, k:k + n].rearrange("p c (a b) -> p c a b", b=nb)
                    ia = idx[:, r, 0, h, a0:a1].unsqueeze(3).to_broadcast([P, nh, a1 - a0, nb])
                    ib = idx[:, r, 1, h, 0:nb].unsqueeze(2).to_broadcast([P, nh, a1 - a0, nb])
                    eng.tensor_tensor(o, ia, ib, ALU.add)
                    k += n
                for c in range(ACT_PAIRS, NP):
                    ins = eng.tensor_scalar(taken(c)[:, h], posu[:, r, h, SKIP[c]:], float(c), None, ALU.is_equal)
                return ins

            def weights(eng, g1):
                wait(eng, slots_mm, g1 * 2)
                eng.tensor_tensor(wslot[:, :, :], ex[:, :, :], einv[:, :].unsqueeze(2).to_broadcast([P, CH, TOP]),
                                  ALU.mult).then_inc(w_done, 1)

            def slot_bank(m0):
                return simp[0] if m0 else slot_p

            TAIL = GROUPS - 2

            DVE_TILES = {TAIL: (0, 1), TAIL + 1: (2, 3)}

            def tail_products(g, c):
                dve_does = c in DVE_TILES[g]
                count = 2 * (g - TAIL) + c % 2 + 1
                return (wg_dve, count) if dve_does else (wg_done, TAIL * TILES + count)

            NB = 8
            TB = COLS // NB

            with nc.Block() as block:
                @block.sync
                def _(sp):
                    def body(s, q):
                        wait(sp, sim_mm[TILES - 1], s - 1)
                        sp.dma_start(xs[:, q, :], xn2T_all[:, bass.ds(s * SEQ, SEQ)]).then_inc(xs_in[q], 16)

                    with sp.Fori(1, GROUPS // 2) as i:
                        for q in range(2):
                            body(i * 2 + q, q)
                    sp.wait_ge(out_sent, 16 * GROUPS)

                @block.tensor
                def _(pe):
                    pe.wait_ge(fold_ev, 2)

                    def model_width(s, g2, tiles):
                        if tiles[0] == 0:
                            wait(pe, fin, g2)
                        for c in tiles:
                            if not tail(s):
                                wait(pe, wg_done, g2 * TILES + c + 1)
                            else:
                                by, count = tail_products(g2, c)
                                pe.wait_ge(by, count)
                            pe.matmul(up_p[:, c * D:(c + 1) * D], ident_w[:, :], x_sb[:, bass.ds(g2 * SEQ + c * P, P)],
                                      start=True, stop=False)
                            for l in range(LO):
                                m = pe.matmul(up_p[:, c * D:(c + 1) * D], wsb[:, l, c * P:(c + 1) * P], up_sb[:, l, :],
                                              start=False, stop=(l == LO - 1))
                        if tiles[-1] == TILES - 1:
                            m.then_inc(up_mm, 1)

                    def body(s, q):
                        g, g1, g2 = s, s - 1, s - 2
                        if active(s, 0):
                            pe.wait_ge(xs_in[q], xs_count(s, q))
                            for c in range(TILES):
                                wait(pe, sim_ev[(c + 2) % TILES], g + 1 if c >= 2 else g)
                                pe.matmul(simp[c % 2][:, :], xs[:, q, c * P:(c + 1) * P], fold_M[:, :], start=True, stop=False)
                                pe.matmul(simp[c % 2][:, :], ones_b[:, :], fold_b[:, :], start=False, stop=True).then_inc(sim_mm[c], 1)
                        for m0, m1 in portions(s):
                            if active(s, 2) and m0 == 0:
                                for l in range(LO):
                                    wait(pe, g_ev, g2 * LO + max(l - 1, 0))
                                    pe.matmul(gp[l % 2][:, :], downT[:, l, :], xn2T_all[:, bass.ds(g2 * SEQ, SEQ)],
                                              start=True, stop=True).then_inc(g_mm, 1)
                            for b in range(m0 * NB // 2, m1 * NB // 2) if active(s, 2) else ():
                                if b == m0 * NB // 2:
                                    wait(pe, built, g2 * 2 + m1)
                                wait(pe, w_ev, g2 * NB + max(b - 1, 0))
                                for t in range(b * TB, (b + 1) * TB):
                                    o = wp[b % 2][:, (t % TB) * 2 * LO:(t % TB + 1) * 2 * LO]
                                    pe.matmul(o, X[:, :, t], Yhi[:, :, t], start=True, stop=False)
                                    m = pe.matmul(o, X[:, :, t], Ylo[:, :, t], start=False, stop=True)
                                m.then_inc(w_mm, 1)
                            if m0:
                                model_width(s, g2, (0, 1))
                            if active(s, 1):
                                wait(pe, e_done, g1 * 2 + m1)
                                wait(pe, w_done, g1 + 1)
                                wait(pe, slots_ev, g1 * 2)
                                if m0:
                                    pe.wait_ge(sim_ev[2], GROUPS)
                                for m2 in range(m0, m1):
                                    for k, src in enumerate((eslot, wslot)):
                                        m = pe.transpose(slot_bank(m0)[:, (2 * k + m2) * P:(2 * k + m2 + 1) * P],
                                                         src[:, 2 * m2 * H:2 * (m2 + 1) * H, :].rearrange("p c k -> p (c k)"), ident[:, :])
                                m.then_inc(slots_mm, m1 - m0)
                        if active(s, 2):
                            model_width(s, g2, (2, 3) if tail(s) else range(TILES))

                    def xs_count(s, q):
                        return (s - q) * 8 + 16

                    steps(pe, 3, body)

                @block.scalar
                def _(act):
                    chain = Chain(act, act_chain)

                    def similarities(g):
                        for c in range(TILES):
                            wait(act, sim_mm[c], g + 1)
                            wait(act, axis_top, g)
                            act.copy(sim[:, c, :, :], simp[c % 2][:, :].rearrange("p (j k) -> p j k", k=NK)).then_inc(sim_ev[c], 1)

                    def body(s, q):
                        g, g1, g2 = s, s - 1, s - 2
                        if active(s, 0) and not (isinstance(s, int) and s == 1):
                            similarities(g)
                        for m0, m1 in portions(s):
                            if active(s, 2) and m0 == 0:
                                if tail(s) and g2 > TAIL:
                                    for c in range(1, TILES, 2):
                                        by, count = tail_products(g2 - 1, c)
                                        act.wait_ge(by, count)
                                else:
                                    wait(act, wg_done, g2 * TILES)
                                for l in range(LO):
                                    wait(act, g_mm, g2 * LO + l + 1)
                                    act.activation(act_g[:, l, :], gp[l % 2][:, :], ACT.Gelu_apprx_tanh).then_inc(g_ev, 1)
                                wait(act, up_mm, g2)
                            for b in range(m0 * NB // 2, m1 * NB // 2) if active(s, 2) else ():
                                wait(act, w_mm, g2 * NB + b + 1)
                                t0 = (b * TB) % P
                                m2 = b * TB // P
                                dst = wsb[:, :, :].rearrange("p l (m r t) -> p m t r l", m=2, r=2)[:, m2, t0:t0 + TB, :, :]
                                act.copy(dst, wp[b % 2][:, :].rearrange("p (t r l) -> p t r l", r=2, l=LO)).then_inc(w_ev, 1)
                            if active(s, 1):
                                n0, n1 = m0 * P, m1 * P
                                bank = slot_bank(m0)
                                E_, W_ = bank[:, n0:n1], bank[:, COLS + n0:COLS + n1]
                                wait(act, slots_mm, g1 * 2 + m1)
                                wait(act, built, g1 * 2)
                                rounded = chain.done(act.activation(sl[:, 0, n0:n1], E_, ACT.Identity, bias=round_up[:, 0:1], scale=1.0 / LO))
                                act.activation(sl[:, 1, n0:n1], E_, ACT.Identity, bias=half_off[:, 0:1])
                                act.activation(whi[:, n0:n1], W_, ACT.Copy, scale=WSCALE)
                                act.activation(sl[:, 2, n0:n1], W_, ACT.Copy, scale=WSCALE)
                                chain.wait(rounded)
                                for j in range(RC):
                                    ins = act.activation(rowid[:, j, n0:n1], sl[:, 0, n0:n1], ACT.Identity, bias=unrow[:, j:j + 1])
                                ins.then_inc(slots_ev, m1 - m0)
                        if active(s, 0):
                            wait(act, axis_top, g + 1)
                            wait(act, e_done, g * 2 - 2)
                            act.activation(idx[:, q, 0, :, :], bidx[:, 0, :, :], ACT.Copy, scale=float(NK))
                            act.activation(idx[:, q, 1, :, :], bidx[:, 1, :, :], ACT.Identity, bias=low_off[:, 0:1]).then_inc(idx_done, 1)
                            if isinstance(s, int) and s == 0:
                                similarities(1)
                            wait(act, ranked, g + 1)
                            wait(act, e_done, g * 2)
                            for c in range(ACT_PAIRS):
                                ins = act.activation(taken(c), posu[:, q, :, SKIP[c]:], ACT.Abs, bias=pair_off[:, c:c + 1])
                            chain.wait(chain.done(ins))
                            o = took[:, 0:PLACE[ACT_PAIRS] * CH]
                            act.activation(o, o, ACT.Relu, bias=one[:, 0:1], scale=-1.0).then_inc(took_done, 1)
                            wait(act, gap_done, g + 1)
                            wait(act, w_done, g)
                            act.activation(ex[:, :, :], gap[:, q, :, :], ACT.Exp).then_inc(exp_done, 1)
                        if active(s, 2):
                            wait(act, up_mm, g2 + 1)
                            act.activation(x_sb[:, bass.ds(g2 * SEQ, SEQ)], up_p[:, :], ACT.Copy, scale=1.0 / WSCALE).then_inc(fin, 1)
                            wait(act, fin, g2 + 1)
                            act.dma_start(out[bass.ds(g2, 1)].rearrange("b (c p) d -> p (b c) d", p=P),
                                          x_sb[:, bass.ds(g2 * SEQ, SEQ)].rearrange("p (c d) -> p c d", d=D)).then_inc(out_sent, 16)
                        chain.restart()

                    steps(act, 3, body)

                @block.gpsimd
                def _(pool):
                    def numbers(g1, r, m0, m1):
                        h = slice(m0 * CH // 2, m1 * CH // 2)
                        nh = h.stop - h.start
                        if isinstance(g1, int) and g1 == 0:
                            pool.wait_ge(first_numbers, 1)
                        else:
                            chain.wait(chain.done(pair_numbers(pool, r, h)))
                        wait(pool, slots_mm, g1 * 2)

                        def add(c, shared, added):
                            chain.wait(max(shared, added))
                            return pool.tensor_tensor(eslot[:, h, SKIP[c]:], eslot[:, h, SKIP[c]:], share[:, c % 3, h, SKIP[c]:], ALU.add)

                        before = None
                        for c in range(NP):
                            if c == 0:
                                wait(pool, took_done, g1 + 1)
                            dst = share[:, c % 3, h, SKIP[c]:] if c else eslot[:, h, :]
                            ins = pool.tensor_tensor(dst, taken(c)[:, h], ecand[:, h, c:c + 1].to_broadcast([P, nh, TOP - SKIP[c]]), ALU.mult)
                            shared = chain.done(ins)
                            added = shared if before is None else chain.done(add(c - 1, before, added))
                            before = shared if c else None
                        add(NP - 1, before, added).then_inc(e_done, m1 - m0)

                    def body(s, q):
                        g1, g2, r = s - 1, s - 2, 1 - q
                        if active(s, 1):
                            wait(pool, ranked, g1 + 1)
                            wait(pool, exp_done, g1 - 1)
                            pool.tensor_tensor(gap[:, r, :, :], top[:, :, :], top[:, :, 0:1].to_broadcast([P, CH, TOP]),
                                               ALU.subtract).then_inc(gap_done, 1)
                        if active(s, 2) and not tail(s):
                            wait(pool, slots_ev, g2 * 2 + 2)
                            wait(pool, built, g2 * 2)
                            pool.tensor_tensor(wlo[:, :], sl[:, 2, :], whi[:, :], ALU.subtract).then_inc(low_done, 1)
                        if active(s, 1):
                            wait(pool, idx_done, g1 + 1)
                            for m0, m1 in portions(s):
                                numbers(g1, r, m0, m1)
                        if not isinstance(s, int):
                            wait(pool, inverted, g1)
                            weights(pool, g1)
                        chain.restart()
                        if active(s, 2):
                            wait(pool, g_ev, (g2 + 1) * LO)
                            for c in range(TILES):
                                if tail(s) and c in DVE_TILES[g2]:
                                    continue
                                wait(pool, w_ev, g2 * NB + NB // 2 * (c // 2 + 1))
                                w = wsb[:, :, c * P:(c + 1) * P]
                                pool.tensor_tensor(w, w, act_g[:, :, c * P:(c + 1) * P], ALU.mult).then_inc(wg_done, 1)

                    chain = Chain(pool, pool_chain)
                    steps(pool, 3, body)

                @block.vector
                def _(dve):
                    chain = Chain(dve, dve_chain)

                    def one_hots(g2, m0, m1):
                        n = slice(m0 * P, m1 * P)
                        wait(dve, slots_ev, g2 * 2 + m1)
                        column = chain.done(dve.scalar_tensor_tensor(out=colid[:, 0, n], in0=rowid[:, 0, n], scalar=-float(LO),
                                                                     in1=sl[:, 1, n], op0=ALU.mult, op1=ALU.add))
                        wait(dve, w_mm, g2 * NB - NB // 2 * (2 - m1))
                        if (m0, m1) != (0, 2):
                            dve.tensor_tensor(wlo[:, n], sl[:, 2, n], whi[:, n], ALU.subtract)
                        chain.wait(column)
                        columns = chain.done(dve.tensor_scalar(colid[:, 1, n], colid[:, 0, n], float(CS), None, ALU.subtract))
                        Xc = X[:, :, n].rearrange("p (j i) t -> p i j t", j=RC)
                        for i in range(RS):
                            dve.tensor_scalar(Xc[:, i], rowid[:, :, n], float(i), None, ALU.is_equal)
                        chain.wait(columns)
                        Yc = Ylo[:, :, n].rearrange("p (j i) t -> p i j t", j=CC)
                        for i in range(CS):
                            ins = dve.tensor_scalar(Yc[:, i], colid[:, :, n], float(i), None, ALU.is_equal)
                        chain.wait(chain.done(ins))
                        shape = [P, 2 * LO, (m1 - m0) * P]
                        dve.tensor_tensor(Yhi[:, :, n], Ylo[:, :, n], whi[:, n].unsqueeze(1).to_broadcast(shape), ALU.mult)
                        if (m0, m1) == (0, 2):
                            wait(dve, low_done, g2 + 1)
                        dve.tensor_tensor(Ylo[:, :, n], Ylo[:, :, n], wlo[:, n].unsqueeze(1).to_broadcast(shape),
                                          ALU.mult).then_inc(built, m1 - m0)

                    def softmax(g1, whole):
                        wait(dve, exp_done, g1 + 1)
                        summed = chain.done(dve.tensor_reduce(esum[:, :], ex[:, :, :], AX.X, ALU.add))
                        wait(dve, w_done, g1)
                        chain.wait(summed)
                        inverse = dve.reciprocal(einv[:, :], esum[:, :])
                        if whole:
                            chain.wait(chain.done(inverse))
                            weights(dve, g1)
                        else:
                            inverse.then_inc(inverted, 1)

                    def products(g2):
                        dve.wait_ge(g_ev, (g2 + 1) * LO)
                        dve.wait_ge(w_ev, g2 * NB + NB // 2 * (DVE_TILES[g2][0] // 2 + 1))
                        for c in DVE_TILES[g2]:
                            w = wsb[:, :, c * P:(c + 1) * P]
                            dve.tensor_tensor(w, w, act_g[:, :, c * P:(c + 1) * P], ALU.mult).then_inc(wg_dve, 1)

                    def body(s, q):
                        g, g1, g2, r = s, s - 1, s - 2, 1 - q
                        for m0, m1 in portions(s) if active(s, 2) else ():
                            one_hots(g2, m0, m1)
                            if tail(s) and m0 == 0 and active(s, 1):
                                softmax(g1, True)
                        early = isinstance(s, int) and s == 1
                        if active(s, 1) and not early and not tail(s):
                            softmax(g1, False)
                        if early:
                            dve.wait_ge(idx_done, 1)
                            dve.wait_ge(ranked, 1)
                            pair_numbers(dve, r, slice(0, CH)).then_inc(first_numbers, 1)
                        if tail(s):
                            products(g2)
                        if active(s, 0):
                            n = 2 * (TILES + 1)
                            touch(dve, idx_done, g, idle[:, n + q:n + q + 1])
                            touch(dve, e_done, g * 2 - 2, idle[:, n + 2 + q:n + 3 + q])
                            touch(dve, gap_done, g, idle[:, n + 4 + q:n + 5 + q])
                            for c in range(TILES):
                                touch(dve, sim_ev[c], g + 1, idle[:, 2 * c + q:2 * c + q + 1])
                                for j in range(HF):
                                    ins = dve.max(best[:, j // H, c * H + j % H, :], sim[:, c, j, :])
                            top_done = chain.done(ins)
                            if early:
                                softmax(g1, True)
                            chain.wait(top_done)
                            for c in range(TILES):
                                for j in range(HF):
                                    ins = dve.max_index(bidx[:, j // H, c * H + j % H, :], best[:, j // H, c * H + j % H, :], sim[:, c, j, :])
                            ins.then_inc(axis_top, 1)
                            k = 0
                            for a0, a1, nb in AROWS:
                                n = (a1 - a0) * nb
                                ins = dve.tensor_tensor(cand[:, :, k:k + n].rearrange("p c (a b) -> p c a b", b=nb),
                                                        best[:, 0, :, a0:a1].unsqueeze(3).to_broadcast([P, CH, a1 - a0, nb]),
                                                        best[:, 1, :, 0:nb].unsqueeze(2).to_broadcast([P, CH, a1 - a0, nb]), ALU.add)
                                k += n
                            sums = chain.done(ins)
                            chain.wait(sums)
                            for m in range(CH):
                                ins = dve.max(top[:, m, :], cand[:, m, :])
                            chain.wait(chain.done(ins))
                            for m in range(CH):
                                ins = dve.max_index(posu[:, q, m, :], top[:, m, :], cand[:, m, :])
                            ins.then_inc(ranked, 1)
                        chain.restart()

                    steps(dve, 3, body)


_INS = ['L0_attn_x', 'L0_attn_W_spec', 'L0_attn_W_decay', 'L0_attn_b_decay', 'L0_attn_freqs', 'L0_attn_W_out',
        'L0_ffn_w_q', 'L0_ffn_bn_gamma', 'L0_ffn_bn_beta', 'L0_ffn_keys', 'L0_ffn_down_embed', 'L0_ffn_up_embed']
_OUTS = [((GROUPS, SEQ, D), 'float32')]


def kernel(**inputs):
    import numpy as _np
    import concourse.bacc as _bacc
    from concourse import mybir as _mybir
    from concourse.bass_utils import run_bass_kernel_spmd as _run

    nc = _bacc.Bacc("TRN2", target_bir_lowering=False, num_devices=1)
    arrays, args = {}, []
    for name in _INS:
        v = _np.ascontiguousarray(inputs[name])
        arrays[f"in_{name}_dram"] = v
        args.append(nc.dram_tensor(f"in_{name}_dram", v.shape, _mybir.dt.from_np(v.dtype), kind="ExternalInput").ap())
    for i, (shape, dtype) in enumerate(_OUTS):
        dt = _mybir.dt.from_np(_np.dtype(dtype))
        args.append(nc.dram_tensor(f"out_{i}_dram", shape, dt, kind="ExternalOutput").ap())
    build(nc, *args)
    r = _run(nc, [arrays], core_ids=[0])
    got = tuple(r.results[0][f"out_{i}_dram"] for i in range(len(_OUTS)))
    return got[0]
```
